# Optimizing a Trainium2 kernel written in Bass

```python
import numpy as np
import jax
import jax.numpy as jnp

def _softmax(x, axis=-1):
    return jax.nn.softmax(x, axis=axis)

def _gelu(x):
    return jax.nn.gelu(x, approximate=True)

def _silu(x):
    return jax.nn.silu(x)

def _sigmoid(x):
    return jax.nn.sigmoid(x)

def _layernorm(x, axis=-1, eps=1e-05):
    m = jnp.mean(x, axis=axis, keepdims=True)
    v = jnp.var(x, axis=axis, keepdims=True)
    return (x - m) / jnp.sqrt(v + eps)

def _scatter_add(tgt, idx, src, axis=0):
    return tgt.at[idx].add(src)

def _segment_sum(src, seg, n):
    return jax.ops.segment_sum(src, seg, n)
kernel_name = 'mk_xattn_seq_d2_seqx_r4_bdbb33'

def setup_inputs(seed: int=0):
    np.random.seed(seed)
    _w = jnp.asarray

    def _rec_inputs():
        import jax
        import jax.numpy as jnp
        _rk = jax.random.key(seed)
        x = -0.0002928 + 1 * jax.random.normal(jax.random.fold_in(_rk, 1), (64, 256, 256), jnp.float32)
        _lenS = 256 - jax.random.randint(jax.random.fold_in(_rk, 7), (64,), 0, max(1, 256 // 4) + 1, jnp.int32)
        _lenS2 = 120 - jax.random.randint(jax.random.fold_in(_rk, 8), (64,), 0, max(1, 120 // 4) + 1, jnp.int32)
        _ctx_1024P = jax.random.normal(jax.random.fold_in(_rk, 11), (64, 16, 256), jnp.float32)
        _ctx_1024c = jax.random.dirichlet(jax.random.fold_in(_rk, 511), 0.3 * jnp.ones((16,), jnp.float32), (64, 120))
        _ctx_1024t = jnp.einsum('bsk,bkd->bsd', _ctx_1024c, _ctx_1024P)
        _ctx_1024t = _ctx_1024t * jax.lax.rsqrt(jnp.mean(jnp.square(_ctx_1024t)) + 1e-12) * 0.953939
        ctx_1024 = -1.39393e-06 + 0.999914 * (_ctx_1024t + 0.3 * jax.random.normal(jax.random.fold_in(_rk, 611), (64, 120, 256), jnp.float32))
        return (x, ctx_1024)
    x, ctx_1024 = _rec_inputs()

    def _L0_xattn_setup():
        import jax, jax.numpy as jnp
        import numpy as np
        B, LQ, LKV = (2, 512, 512)
        DQ, DKV, HID, NH = (256, 256, 256, 16)
        HD = HID // NH
        EPS = 1e-05
        key = jax.random.key(seed)
        ks = jax.random.split(key, 12)
        s_q = 1.0 / np.sqrt(DQ)
        s_kv = 1.0 / np.sqrt(DKV)
        s_h = 1.0 / np.sqrt(HID)
        return {'query': jax.random.normal(ks[0], (B, LQ, DQ), jnp.float32), 'key_value': jax.random.normal(ks[1], (B, LKV, DKV), jnp.float32), 'Wq': jax.random.uniform(ks[2], (DQ, HID), jnp.float32, -s_q, s_q), 'bq': jax.random.uniform(ks[3], (HID,), jnp.float32, -s_q, s_q), 'Wk': jax.random.uniform(ks[4], (DKV, HID), jnp.float32, -s_kv, s_kv), 'bk': jax.random.uniform(ks[5], (HID,), jnp.float32, -s_kv, s_kv), 'Wv': jax.random.uniform(ks[6], (DKV, HID), jnp.float32, -s_kv, s_kv), 'bv': jax.random.uniform(ks[7], (HID,), jnp.float32, -s_kv, s_kv), 'Wo': jax.random.uniform(ks[8], (HID, DQ), jnp.float32, -s_h, s_h), 'bo': jax.random.uniform(ks[9], (DQ,), jnp.float32, -s_h, s_h), 'ln_gamma': jnp.ones((DQ,), jnp.float32), 'ln_beta': jnp.zeros((DQ,), jnp.float32)}
    _L0_xattn_all = _L0_xattn_setup()
    _L0_xattn_in = {k: v for k, v in _L0_xattn_all.items() if k in ('Wq', 'bq', 'Wk', 'bk', 'Wv', 'bv', 'Wo', 'bo', 'ln_gamma', 'ln_beta')}
    del _L0_xattn_all

    def _L1_xattn_setup():
        import jax, jax.numpy as jnp
        import numpy as np
        D, H, DFF, MD = (256, 16, 1024, 128)
        B, TS, TT = (8, 128, 128)
        EPS = 1e-06

        def _ln(x, s, b):
            m = jnp.mean(x, axis=-1, keepdims=True)
            v = jnp.mean((x - m) ** 2, axis=-1, keepdims=True)
            return (x - m) * jax.lax.rsqrt(v + EPS) * s + b

        def _rel_bias(emb, qlen, klen):
            q = jnp.arange(qlen)[:, None]
            k = jnp.arange(klen)[None, :]
            rp = k - q
            bucket = jnp.where(rp < 0, jnp.minimum(-rp, MD - 1), jnp.minimum(rp, MD - 1) + MD)
            return emb[bucket].transpose(2, 0, 1)

        def _mha(xq, xkv, w_in, b_in, w_out, b_out, bias):
            Bq, Tq, _ = xq.shape
            Tk = xkv.shape[1]
            hd = D // H
            wq, wk, wv = jnp.split(w_in, 3, axis=0)
            bq, bk, bv = jnp.split(b_in, 3, axis=0)
            q = (xq @ wq.T + bq).reshape(Bq, Tq, H, hd).transpose(0, 2, 1, 3)
            k = (xkv @ wk.T + bk).reshape(Bq, Tk, H, hd).transpose(0, 2, 1, 3)
            v = (xkv @ wv.T + bv).reshape(Bq, Tk, H, hd).transpose(0, 2, 1, 3)
            scores = jnp.einsum('bhqd,bhkd->bhqk', q, k) / jnp.sqrt(jnp.asarray(hd, xq.dtype))
            scores = scores + bias[None]
            attn = jax.nn.softmax(scores, axis=-1)
            out = jnp.einsum('bhqk,bhkd->bhqd', attn, v)
            out = out.transpose(0, 2, 1, 3).reshape(Bq, Tq, D)
            return out @ w_out.T + b_out
        key = jax.random.key(seed)
        ks = jax.random.split(key, 40)
        std = 0.02

        def n(i, shape):
            return jax.random.normal(ks[i], shape, dtype=jnp.float32) * std
        return {'src': jax.random.normal(ks[0], (B, TS, D), dtype=jnp.float32), 'tgt': jax.random.normal(ks[1], (B, TT, D), dtype=jnp.float32), 'enc_in_w': n(2, (3 * D, D)), 'enc_in_b': jnp.zeros((3 * D,)), 'enc_out_w': n(3, (D, D)), 'enc_out_b': jnp.zeros((D,)), 'enc_ff1_w': n(4, (DFF, D)), 'enc_ff1_b': jnp.zeros((DFF,)), 'enc_ff2_w': n(5, (D, DFF)), 'enc_ff2_b': jnp.zeros((D,)), 'enc_n1_s': jnp.ones((D,)), 'enc_n1_b': jnp.zeros((D,)), 'enc_n2_s': jnp.ones((D,)), 'enc_n2_b': jnp.zeros((D,)), 'enc_rel': n(6, (2 * MD, H)), 'dec_sa_in_w': n(7, (3 * D, D)), 'dec_sa_in_b': jnp.zeros((3 * D,)), 'dec_sa_out_w': n(8, (D, D)), 'dec_sa_out_b': jnp.zeros((D,)), 'dec_ca_in_w': n(9, (3 * D, D)), 'dec_ca_in_b': jnp.zeros((3 * D,)), 'dec_ca_out_w': n(10, (D, D)), 'dec_ca_out_b': jnp.zeros((D,)), 'dec_ff1_w': n(11, (DFF, D)), 'dec_ff1_b': jnp.zeros((DFF,)), 'dec_ff2_w': n(12, (D, DFF)), 'dec_ff2_b': jnp.zeros((D,)), 'dec_n1_s': jnp.ones((D,)), 'dec_n1_b': jnp.zeros((D,)), 'dec_n2_s': jnp.ones((D,)), 'dec_n2_b': jnp.zeros((D,)), 'dec_n3_s': jnp.ones((D,)), 'dec_n3_b': jnp.zeros((D,)), 'dec_rel_self': n(13, (2 * MD, H)), 'dec_rel_cross': n(14, (2 * MD, H))}
    _L1_xattn_all = _L1_xattn_setup()
    _L1_xattn_in = {k: v for k, v in _L1_xattn_all.items() if k in ('enc_in_w', 'enc_in_b', 'enc_out_w', 'enc_out_b', 'enc_ff1_w', 'enc_ff1_b', 'enc_ff2_w', 'enc_ff2_b', 'enc_n1_s', 'enc_n1_b', 'enc_n2_s', 'enc_n2_b', 'enc_rel', 'dec_sa_in_w', 'dec_sa_in_b', 'dec_sa_out_w', 'dec_sa_out_b', 'dec_ca_in_w', 'dec_ca_in_b', 'dec_ca_out_w', 'dec_ca_out_b', 'dec_ff1_w', 'dec_ff1_b', 'dec_ff2_w', 'dec_ff2_b', 'dec_n1_s', 'dec_n1_b', 'dec_n2_s', 'dec_n2_b', 'dec_n3_s', 'dec_n3_b', 'dec_rel_self', 'dec_rel_cross')}
    del _L1_xattn_all
    return {'x': x, 'ctx_1024': ctx_1024, 'L0_xattn_Wq': _L0_xattn_in['Wq'], 'L0_xattn_bq': _L0_xattn_in['bq'], 'L0_xattn_Wk': _L0_xattn_in['Wk'], 'L0_xattn_bk': _L0_xattn_in['bk'], 'L0_xattn_Wv': _L0_xattn_in['Wv'], 'L0_xattn_bv': _L0_xattn_in['bv'], 'L0_xattn_Wo': _L0_xattn_in['Wo'], 'L0_xattn_bo': _L0_xattn_in['bo'], 'L0_xattn_ln_gamma': _L0_xattn_in['ln_gamma'], 'L0_xattn_ln_beta': _L0_xattn_in['ln_beta'], 'L1_xattn_enc_in_w': _L1_xattn_in['enc_in_w'], 'L1_xattn_enc_in_b': _L1_xattn_in['enc_in_b'], 'L1_xattn_enc_out_w': _L1_xattn_in['enc_out_w'], 'L1_xattn_enc_out_b': _L1_xattn_in['enc_out_b'], 'L1_xattn_enc_ff1_w': _L1_xattn_in['enc_ff1_w'], 'L1_xattn_enc_ff1_b': _L1_xattn_in['enc_ff1_b'], 'L1_xattn_enc_ff2_w': _L1_xattn_in['enc_ff2_w'], 'L1_xattn_enc_ff2_b': _L1_xattn_in['enc_ff2_b'], 'L1_xattn_enc_n1_s': _L1_xattn_in['enc_n1_s'], 'L1_xattn_enc_n1_b': _L1_xattn_in['enc_n1_b'], 'L1_xattn_enc_n2_s': _L1_xattn_in['enc_n2_s'], 'L1_xattn_enc_n2_b': _L1_xattn_in['enc_n2_b'], 'L1_xattn_enc_rel': _L1_xattn_in['enc_rel'], 'L1_xattn_dec_sa_in_w': _L1_xattn_in['dec_sa_in_w'], 'L1_xattn_dec_sa_in_b': _L1_xattn_in['dec_sa_in_b'], 'L1_xattn_dec_sa_out_w': _L1_xattn_in['dec_sa_out_w'], 'L1_xattn_dec_sa_out_b': _L1_xattn_in['dec_sa_out_b'], 'L1_xattn_dec_ca_in_w': _L1_xattn_in['dec_ca_in_w'], 'L1_xattn_dec_ca_in_b': _L1_xattn_in['dec_ca_in_b'], 'L1_xattn_dec_ca_out_w': _L1_xattn_in['dec_ca_out_w'], 'L1_xattn_dec_ca_out_b': _L1_xattn_in['dec_ca_out_b'], 'L1_xattn_dec_ff1_w': _L1_xattn_in['dec_ff1_w'], 'L1_xattn_dec_ff1_b': _L1_xattn_in['dec_ff1_b'], 'L1_xattn_dec_ff2_w': _L1_xattn_in['dec_ff2_w'], 'L1_xattn_dec_ff2_b': _L1_xattn_in['dec_ff2_b'], 'L1_xattn_dec_n1_s': _L1_xattn_in['dec_n1_s'], 'L1_xattn_dec_n1_b': _L1_xattn_in['dec_n1_b'], 'L1_xattn_dec_n2_s': _L1_xattn_in['dec_n2_s'], 'L1_xattn_dec_n2_b': _L1_xattn_in['dec_n2_b'], 'L1_xattn_dec_n3_s': _L1_xattn_in['dec_n3_s'], 'L1_xattn_dec_n3_b': _L1_xattn_in['dec_n3_b'], 'L1_xattn_dec_rel_self': _L1_xattn_in['dec_rel_self'], 'L1_xattn_dec_rel_cross': _L1_xattn_in['dec_rel_cross']}

def reference(x, ctx_1024, L0_xattn_Wq, L0_xattn_bq, L0_xattn_Wk, L0_xattn_bk, L0_xattn_Wv, L0_xattn_bv, L0_xattn_Wo, L0_xattn_bo, L0_xattn_ln_gamma, L0_xattn_ln_beta, L1_xattn_enc_in_w, L1_xattn_enc_in_b, L1_xattn_enc_out_w, L1_xattn_enc_out_b, L1_xattn_enc_ff1_w, L1_xattn_enc_ff1_b, L1_xattn_enc_ff2_w, L1_xattn_enc_ff2_b, L1_xattn_enc_n1_s, L1_xattn_enc_n1_b, L1_xattn_enc_n2_s, L1_xattn_enc_n2_b, L1_xattn_enc_rel, L1_xattn_dec_sa_in_w, L1_xattn_dec_sa_in_b, L1_xattn_dec_sa_out_w, L1_xattn_dec_sa_out_b, L1_xattn_dec_ca_in_w, L1_xattn_dec_ca_in_b, L1_xattn_dec_ca_out_w, L1_xattn_dec_ca_out_b, L1_xattn_dec_ff1_w, L1_xattn_dec_ff1_b, L1_xattn_dec_ff2_w, L1_xattn_dec_ff2_b, L1_xattn_dec_n1_s, L1_xattn_dec_n1_b, L1_xattn_dec_n2_s, L1_xattn_dec_n2_b, L1_xattn_dec_n3_s, L1_xattn_dec_n3_b, L1_xattn_dec_rel_self, L1_xattn_dec_rel_cross):
    import jax
    import jax.numpy as jnp

    def _L0_xattn_ref(query, key_value, Wq, bq, Wk, bk, Wv, bv, Wo, bo, ln_gamma, ln_beta):
        import jax, jax.numpy as jnp
        import numpy as np
        B, LQ, LKV = (2, 512, 512)
        DQ, DKV, HID, NH = (256, 256, 256, 16)
        HD = HID // NH
        EPS = 1e-05
        b, lq, _ = query.shape
        lkv = key_value.shape[1]
        Q = (query @ Wq + bq).reshape(b, lq, NH, HD).transpose(0, 2, 1, 3)
        K = (key_value @ Wk + bk).reshape(b, lkv, NH, HD).transpose(0, 2, 1, 3)
        V = (key_value @ Wv + bv).reshape(b, lkv, NH, HD).transpose(0, 2, 1, 3)
        scores = jnp.einsum('bhqd,bhkd->bhqk', Q, K) / jnp.sqrt(jnp.float32(HD))
        attn = jax.nn.softmax(scores, axis=-1)
        ctx = jnp.einsum('bhqk,bhkd->bhqd', attn, V)
        ctx = ctx.transpose(0, 2, 1, 3).reshape(b, lq, HID)
        out = ctx @ Wo + bo
        x = query + out
        mu = jnp.mean(x, axis=-1, keepdims=True)
        var = jnp.mean(jnp.square(x - mu), axis=-1, keepdims=True)
        return (x - mu) / jnp.sqrt(var + EPS) * ln_gamma + ln_beta

    def _L1_xattn_ref(src, tgt, enc_in_w, enc_in_b, enc_out_w, enc_out_b, enc_ff1_w, enc_ff1_b, enc_ff2_w, enc_ff2_b, enc_n1_s, enc_n1_b, enc_n2_s, enc_n2_b, enc_rel, dec_sa_in_w, dec_sa_in_b, dec_sa_out_w, dec_sa_out_b, dec_ca_in_w, dec_ca_in_b, dec_ca_out_w, dec_ca_out_b, dec_ff1_w, dec_ff1_b, dec_ff2_w, dec_ff2_b, dec_n1_s, dec_n1_b, dec_n2_s, dec_n2_b, dec_n3_s, dec_n3_b, dec_rel_self, dec_rel_cross):
        import jax, jax.numpy as jnp
        import numpy as np
        D, H, DFF, MD = (256, 16, 1024, 128)
        B, TS, TT = (8, 128, 128)
        EPS = 1e-06

        def _ln(x, s, b):
            m = jnp.mean(x, axis=-1, keepdims=True)
            v = jnp.mean((x - m) ** 2, axis=-1, keepdims=True)
            return (x - m) * jax.lax.rsqrt(v + EPS) * s + b

        def _rel_bias(emb, qlen, klen):
            q = jnp.arange(qlen)[:, None]
            k = jnp.arange(klen)[None, :]
            rp = k - q
            bucket = jnp.where(rp < 0, jnp.minimum(-rp, MD - 1), jnp.minimum(rp, MD - 1) + MD)
            return emb[bucket].transpose(2, 0, 1)

        def _mha(xq, xkv, w_in, b_in, w_out, b_out, bias):
            Bq, Tq, _ = xq.shape
            Tk = xkv.shape[1]
            hd = D // H
            wq, wk, wv = jnp.split(w_in, 3, axis=0)
            bq, bk, bv = jnp.split(b_in, 3, axis=0)
            q = (xq @ wq.T + bq).reshape(Bq, Tq, H, hd).transpose(0, 2, 1, 3)
            k = (xkv @ wk.T + bk).reshape(Bq, Tk, H, hd).transpose(0, 2, 1, 3)
            v = (xkv @ wv.T + bv).reshape(Bq, Tk, H, hd).transpose(0, 2, 1, 3)
            scores = jnp.einsum('bhqd,bhkd->bhqk', q, k) / jnp.sqrt(jnp.asarray(hd, xq.dtype))
            scores = scores + bias[None]
            attn = jax.nn.softmax(scores, axis=-1)
            out = jnp.einsum('bhqk,bhkd->bhqd', attn, v)
            out = out.transpose(0, 2, 1, 3).reshape(Bq, Tq, D)
            return out @ w_out.T + b_out
        Ts, Tt = (src.shape[1], tgt.shape[1])
        eb = _rel_bias(enc_rel, Ts, Ts)
        x = src
        x = x + _mha(_ln(x, enc_n1_s, enc_n1_b), _ln(x, enc_n1_s, enc_n1_b), enc_in_w, enc_in_b, enc_out_w, enc_out_b, eb)
        h = _ln(x, enc_n2_s, enc_n2_b)
        x = x + (jax.nn.relu(h @ enc_ff1_w.T + enc_ff1_b) @ enc_ff2_w.T + enc_ff2_b)
        memory = x
        causal = jnp.where(jnp.arange(Tt)[None, :] > jnp.arange(Tt)[:, None], -jnp.inf, 0.0)
        sb = _rel_bias(dec_rel_self, Tt, Tt) + causal[None]
        cb = _rel_bias(dec_rel_cross, Tt, Ts)
        y = tgt
        yn = _ln(y, dec_n1_s, dec_n1_b)
        y = y + _mha(yn, yn, dec_sa_in_w, dec_sa_in_b, dec_sa_out_w, dec_sa_out_b, sb)
        y = y + _mha(_ln(y, dec_n2_s, dec_n2_b), memory, dec_ca_in_w, dec_ca_in_b, dec_ca_out_w, dec_ca_out_b, cb)
        h = _ln(y, dec_n3_s, dec_n3_b)
        y = y + (jax.nn.relu(h @ dec_ff1_w.T + dec_ff1_b) @ dec_ff2_w.T + dec_ff2_b)
        return y
    x = _L0_xattn_ref(x, ctx_1024, L0_xattn_Wq, L0_xattn_bq, L0_xattn_Wk, L0_xattn_bk, L0_xattn_Wv, L0_xattn_bv, L0_xattn_Wo, L0_xattn_bo, L0_xattn_ln_gamma, L0_xattn_ln_beta)
    x = _L1_xattn_ref(ctx_1024, x, L1_xattn_enc_in_w, L1_xattn_enc_in_b, L1_xattn_enc_out_w, L1_xattn_enc_out_b, L1_xattn_enc_ff1_w, L1_xattn_enc_ff1_b, L1_xattn_enc_ff2_w, L1_xattn_enc_ff2_b, L1_xattn_enc_n1_s, L1_xattn_enc_n1_b, L1_xattn_enc_n2_s, L1_xattn_enc_n2_b, L1_xattn_enc_rel, L1_xattn_dec_sa_in_w, L1_xattn_dec_sa_in_b, L1_xattn_dec_sa_out_w, L1_xattn_dec_sa_out_b, L1_xattn_dec_ca_in_w, L1_xattn_dec_ca_in_b, L1_xattn_dec_ca_out_w, L1_xattn_dec_ca_out_b, L1_xattn_dec_ff1_w, L1_xattn_dec_ff1_b, L1_xattn_dec_ff2_w, L1_xattn_dec_ff2_b, L1_xattn_dec_n1_s, L1_xattn_dec_n1_b, L1_xattn_dec_n2_s, L1_xattn_dec_n2_b, L1_xattn_dec_n3_s, L1_xattn_dec_n3_b, L1_xattn_dec_rel_self, L1_xattn_dec_rel_cross)
    return x

_drawn_inputs = setup_inputs


def setup_inputs(seed=0):
    import zlib

    import numpy as np

    out = dict(_drawn_inputs(seed))
    spreads = {'L0_xattn_ln_gamma': (1.0, 0.2),
     'L0_xattn_ln_beta': (0.0, 0.1),
     'L1_xattn_enc_in_b': (0.0, 0.8),
     'L1_xattn_enc_out_b': (0.0, 0.8),
     'L1_xattn_enc_ff1_b': (0.0, 0.8),
     'L1_xattn_enc_ff2_b': (0.0, 0.74),
     'L1_xattn_enc_n1_s': (1.0, 0.6),
     'L1_xattn_enc_n1_b': (0.0, 0.8),
     'L1_xattn_enc_n2_s': (1.0, 0.6),
     'L1_xattn_enc_n2_b': (0.0, 0.8),
     'L1_xattn_dec_sa_in_b': (0.0, 0.268),
     'L1_xattn_dec_sa_out_b': (0.0, 0.1),
     'L1_xattn_dec_ca_in_b': (0.0, 0.277),
     'L1_xattn_dec_ca_out_b': (0.0, 0.1),
     'L1_xattn_dec_ff1_b': (0.0, 0.302),
     'L1_xattn_dec_ff2_b': (0.0, 0.1),
     'L1_xattn_dec_n1_s': (1.0, 0.6),
     'L1_xattn_dec_n1_b': (0.0, 0.8),
     'L1_xattn_dec_n2_s': (1.0, 0.6),
     'L1_xattn_dec_n2_b': (0.0, 0.8),
     'L1_xattn_dec_n3_s': (1.0, 0.6),
     'L1_xattn_dec_n3_b': (0.0, 0.623)}
    factors = {'L0_xattn_Wq': 2.745,
     'L0_xattn_bq': 8.0,
     'L0_xattn_Wk': 2.734,
     'L0_xattn_bk': 200.0,
     'L0_xattn_bv': 2.944,
     'L1_xattn_enc_in_w': 8.0,
     'L1_xattn_enc_out_w': 8.0,
     'L1_xattn_enc_ff1_w': 8.0,
     'L1_xattn_enc_ff2_w': 4.584,
     'L1_xattn_enc_rel': 51.679,
     'L1_xattn_dec_rel_self': 200.0,
     'L1_xattn_dec_rel_cross': 31.126}
    for name, (base, spread) in spreads.items():
        noise = np.random.default_rng([zlib.crc32(name.encode()), seed]).standard_normal(out[name].shape)
        drawn = base * np.exp(spread * noise) if base else spread * noise
        out[name] = jnp.asarray(drawn.astype(out[name].dtype))
    for name, factor in factors.items():
        out[name] = (out[name] * factor).astype(out[name].dtype)
    return out
```

```python
from contextlib import ExitStack

import concourse.bass as bass
from concourse import mybir

F32 = mybir.dt.float32
F32R = mybir.dt.float32r
BF16 = mybir.dt.bfloat16
ALU = mybir.AluOpType
ACT = mybir.ActivationFunctionType
AX = mybir.AxisListType

NB, LQ, D = 64, 256, 256
LK = 120
H, HD = 16, 16
DFF = 1024
P = 128
KC = D // P
G = 2
IT = NB // G
TQ = LQ // P
TD = G * TQ
ND = G * LQ
NE = G * LK
FC = DFF // P
SCALE = 1.0 / HD ** 0.5
MASKED = -1.0e30
EPS_L0, EPS_L1 = 1e-5, 1e-6
ENC, XA, SA, CA = range(4)

COLS = ["enc_bq", "enc_bk", "xa_bq", "xa_bk", "sa_bq", "sa_bk", "ca_bq", "ca_bk",
        "enc_n1_s", "enc_n1_b", "enc_n2_s", "enc_n2_b",
        "dec_n1_s", "dec_n1_b", "dec_n2_s", "dec_n2_b", "dec_n3_s", "dec_n3_b"]
COL = {name: KC * i for i, name in enumerate(COLS)}
COL["enc_ff1"] = KC * len(COLS)
COL["dec_ff1"] = COL["enc_ff1"] + FC
NCOL = COL["dec_ff1"] + FC
ROWS = ["enc_bv", "enc_bo", "enc_ff2", "xa_bv", "xa_bo", "gamma", "beta", "sa_bv", "sa_bo", "ca_bv", "ca_bo", "dec_ff2"]
ROW = {name: i for i, name in enumerate(ROWS)}
PRE = ["enc", "xa", "sa", "ca"]
LINE = 384


def queries(a):
    return LK if a == ENC else LQ


def units(a):
    out = []
    for pair in range(2):
        if a == ENC:
            out += [(2 * pair + r, 0, 4, 0, 0, LK) for r in range(2)]
        else:
            out += [(2 * pair + r, v, 2, 0, 0, LQ) for v in (0, 2) for r in range(2)]
        if a == SA:
            out += [(2 * pair + r, 0, 4, 1, P, LQ - P) for r in range(2)]
    return out


def max_tiles(a):
    if a == ENC:
        return [(0, g, 0, 4, LK) for g in range(4)]
    if a != SA:
        return [(t, g, 0, 4, LK) for t in range(TQ) for g in range(4)]
    return ([(0, g, 0, 4, P) for g in range(4)]
            + [(1, 2 * c + r, v, 2, 2 * P) for c in range(2) for v in (0, 2) for r in range(2)])


def steps(a):
    n0, n1 = 2 * a, 2 * a + 1
    U = len(units(a))
    per = U // 2
    qt = 1 if a == ENC else TQ
    out = [("k", n0)] if a == SA else [("k", a)]
    out += [("mx", n0), ("mt", n0)]
    if a != SA:
        out += [("mx", n1), ("mt", n1)]
    lag = min(2, per)
    todo = []
    for n in (n0, n1):
        if a == SA and n == n1:
            out += [("k", n1), ("mx", n1), ("mt", n1)]
        for u in range(U):
            out.append(("st", n, u))
            if u == 1 and n == n1:
                out += [("pv", n0, 1)] + [("tq", n0, t) for t in range(qt)]
            if u == 3 and n == n1:
                out.append(("tc", n0))
            if u == per - 1 + lag and (a != ENC or True):
                out.append(("pv", n, 0))
    out += [("pv", n1, 1)] + [("tq", n1, t) for t in range(qt)] + [("tc", n1)]
    return out


def gp_uses():
    out = [("ct", "act"), ("et", "act"), (("xt", 0), "act"), (("xt", 1), "act")]

    def attention(a):
        o = [(("q", a, c), "act") for c in range(1 if a == ENC else KC)]
        o += [(("v", a, j), "dve") for j in range(2 if a == SA else 1)]
        for s in steps(a):
            if s[0] == "k":
                o.append((s, "dve"))
            elif s[0] == "mt":
                o.append((s, "act"))
            elif s[0] == "tq":
                o.append((s, "dve"))
            elif s[0] == "tc":
                o.append((s, "act"))
        return o

    out += attention(ENC) + [(("o", ENC, 0), "dve")] + attention(XA)
    out += [(("o", XA, j), "dve") for j in range(2)]
    out += [("ht", "act")] + [(("f1e", j), "act") for j in range(FC // 2)] + [("f2e", "dve"), ("mem", "act")]
    out += [(("yt", SA, c), "act") for c in range(KC)]
    out += attention(SA) + [(("o", SA, j), "dve") for j in range(2)]
    out += [(("yt", CA, c), "act") for c in range(KC)]
    out += attention(CA) + [(("o", CA, j), "dve") for j in range(2)]
    out += [(("yt", "ff", c), "act") for c in range(KC)]
    out += [(("f1d", j), "act") for j in range(FC)] + [(("f2d", j), "dve") for j in range(2)]
    return out


def build(nc, x, ctxt, wm, wff1, wff2, cols, rows, rel_up, rel_down, out):
    with ExitStack() as stack:
        def sb(name, shape, dt=F32):
            return stack.enter_context(nc.sbuf_tensor(name, shape, dt))

        def ps(name, shape):
            return stack.enter_context(nc.psum_tensor(name, shape, F32))

        def sem(name):
            return stack.enter_context(nc.semaphore(name))

        w_sb = sb("w_sb", [P, 16, KC, D])
        ff1_sb = sb("ff1_sb", [P, 2, KC, DFF])
        ff2_sb = sb("ff2_sb", [P, 2, FC, D])
        col_sb = sb("col_sb", [P, NCOL])
        row_sb = sb("row_sb", [P, len(ROWS), D])
        ident = sb("ident", [P, P])
        identb = sb("identb", [P, P], BF16)
        head_mask = sb("head_mask", [P, 4])
        pick = sb("pick", [P, 8, P], BF16)
        exponent = sb("exponent", [P, TD])
        tk = {ENC: sb("tk_enc", [P, H, LK]), SA: sb("tk_sa", [P, H, LQ]), CA: sb("tk_ca", [P, H, LQ])}
        tq = {ENC: sb("tq_enc", [P, H, LK], BF16), SA: sb("tq_sa", [P, H, LQ], BF16), CA: sb("tq_ca", [P, H, LQ], BF16)}
        X = sb("X", [P, TD, D])
        C = sb("C", [P, G, D])
        CT = sb("CT", [P, KC, NE])
        ET = sb("ET", [P, KC, NE])
        DT = sb("DT", [P, KC, ND])
        XE = sb("XE", [P, G, D])
        XN = sb("XN", [P, TD, D])
        OC = XN
        CN = sb("CN", [P, TQ, D])
        QT = sb("QT", [P, KC, ND])
        QR = sb("QR", [P, KC, ND], F32R)
        KM = sb("KM", [P, KC, 4, LQ])
        KR = sb("KR", [P, KC, 4, LQ], F32R)
        V = sb("V", [P, 4, H, HD + 1])
        PR = sb("PR", [P, 8, 512])
        HID = PR
        NM = sb("NM", [P, 2, TQ, P])
        MT = sb("MT", [P, 2, LQ], BF16)
        st6 = sb("st6", [P, TD, 6])
        mv = sb("mv", [P, TD, 2])
        ve = sb("ve", [P, TD])
        rstd = sb("rstd", [P, TD])
        rden = sb("rden", [P, 2, H])
        GP = ps("GP", [P, 2, 512])
        MX = ps("MX", [P, 2, 512])
        ST = ps("ST", [P, 2, 512])
        OT = ps("OT", [P, 4, LQ])

        lines = nc.dram_tensor("lines", [6, H, LINE], F32, kind="Internal").ap()

        uses = gp_uses()
        use_of = {lab: i for i, (lab, _) in enumerate(uses)}
        attn = [(a, n) for a in range(4) for n in (2 * a, 2 * a + 1)]
        unit_list = [(n, u) for a, n in attn for u in range(len(units(a)))]
        unit_of = {x: i for i, x in enumerate(unit_list)}
        assert len(unit_list) % 8 == 0
        biased = [(n, u) for n, u in unit_list if n // 2 != XA]
        mx_list = [(n, i) for a, n in attn for i in range(len(max_tiles(a)))]
        assert all(len(max_tiles(a)) % 2 == 0 for a in range(4))

        def last_reader(i):
            if i < 8:
                return None
            n, u = unit_list[i - 8]
            return n, 2 * u // len(units(n // 2))

        lns = ["E1", "E2", "L0", "D1", "D2", "D3"]
        ln_tiles = {x: (G if x[0] == "E" else TD) for x in lns}
        ln_order = ["E1", "E2", "L0", "D1", "D2", "D3"]

        def signal(name, labels):
            return {"sem": sem(name), "at": {x: i + 1 for i, x in enumerate(labels)}, "n": len(labels)}

        gp_full = signal("gp_full", [lab for lab, _ in uses])
        act_gp = signal("act_gp", [lab for lab, e in uses if e == "act"])
        dve_gp = signal("dve_gp", [lab for lab, e in uses if e == "dve"])
        mx_full = signal("mx_full", mx_list)
        mx_done = signal("mx_done", mx_list)
        st_full = signal("st_full", unit_list)
        st_biased = signal("st_biased", biased)
        p_ready = signal("p_ready", unit_list)
        pv_done = signal("pv_done", [(n, p) for _, n in attn for p in range(2)])
        oc_ready = signal("oc_ready", [(n, p) for _, n in attn for p in range(2)])
        tq_list = [("tq", n, t) for a, n in attn for t in range(1 if a == ENC else TQ)]
        den_ready = signal("den_ready", tq_list)
        kr_ready = signal("kr_ready", [(s, c) for a in range(4) for s in steps(a) if s[0] == "k" for c in range(KC)])
        qr_ready = signal("qr_ready", [(a, c) for a in range(4) for c in range(KC)])
        stats = signal("stats", [(l, t) for l in ln_order for t in range(ln_tiles[l])])
        aggr = signal("aggr", [(l, t) for l in ln_order for t in range(ln_tiles[l])])
        eps_added = signal("eps_added", ln_order)
        rstd_ready = signal("rstd_ready", ln_order)
        xn_ready = signal("xn_ready", [(l, t) for l in ln_order for t in range(ln_tiles[l])])
        l0_affine = signal("l0_affine", ["gamma", "beta"])
        pre_added = signal("pre_added", ["enc_bo", "xa_bo", "enc_ff2", "sa_bo", "ca_bo", "dec_ff2"])
        c_loaded, x_loaded, stored = sem("c_loaded"), sem("x_loaded"), sem("stored")
        w_loaded, built, lines_out, toep = sem("w_loaded"), sem("built"), sem("lines_out"), sem("toep")
        made, ident_made, flip_made = sem("made"), sem("ident_made"), sem("flip_made")
        flip_full, flip_out, zeroed = sem("flip_full"), sem("flip_out"), sem("zeroed")

        settled = {nc.vector: sem("dve_settled"), nc.gpsimd: sem("pool_settled"), nc.sync: sem("sp_settled")}

        block = stack.enter_context(nc.Block())

        def wait(eng, sig, label, it):
            eng.wait_ge(sig["sem"], it * sig["n"] + sig["at"][label])

        def settle(eng):
            eng.sem_inc(settled[eng], 1)

        def col(name, c, p=P):
            return col_sb[0:p, COL[name] + c:COL[name] + c + 1]

        def bank(label):
            return GP[:, use_of[label] % 2, :]

        N_CONST_DMA = 12
        REL = [ENC, SA, CA]
        rel_sb = PR[0:H, 0:3, :].rearrange("h r (d e) -> h r d e", d=2)
        staging = PR[:].rearrange("p s n -> p (s n)")
        homes = [b[0:H].rearrange("h c n -> h (c n)") for b in (XN, QT, DT)]

        tables = []
        for a in REL:
            w = LK if a == ENC else LQ
            tables += [(a, tk[a], w, 0), (a, tq[a], w, P if a == ENC else 0)]
        flip = CN[:, 0, 0:P]

        def table_blocks(w):
            return H * w // (4 * w if w == LK else 2 * w)

        N_FLIP = sum(table_blocks(w) for _, _, w, _ in tables)

        def line(i):
            return homes[i // 2][:, LINE * (i % 2):LINE * (i % 2 + 1)]

        @block.sync
        def _(sp):
            sp.dma_start(w_sb[:].rearrange("p m c n -> p m (c n)"), wm).then_inc(w_loaded, 16)
            sp.dma_start(ff1_sb[:].rearrange("p m c n -> p m (c n)"), wff1).then_inc(w_loaded, 16)
            sp.dma_start(ff2_sb[:].rearrange("p m c n -> p m (c n)"), wff2).then_inc(w_loaded, 16)
            sp.dma_start(col_sb[:], cols).then_inc(w_loaded, 16)
            sp.dma_start(row_sb[:].rearrange("p r d -> p (r d)"),
                         bass.AP(rows.tensor, 0, [[0, P], [1, len(ROWS) * D]])).then_inc(w_loaded, 16)
            for r in range(3):
                sp.dma_start(rel_sb[:, r, 0, :], rel_up[r]).then_inc(toep, 16)
                sp.dma_start(rel_sb[:, r, 1, :], rel_down[r]).then_inc(toep, 16)
            sp.wait_ge(built, 6)
            for i in range(6):
                sp.dma_start(lines[i], line(i)).then_inc(lines_out, 16)
            sp.wait_ge(lines_out, 96)
            done = 0
            for j, (a, tab, w, off) in enumerate(tables):
                if j:
                    sp.wait_ge(flip_out, done)
                sp.dma_start(staging[:, 0:H * w].rearrange("p (h w) -> p h w", h=H),
                             bass.AP(lines.tensor, j * H * LINE + off, [[1, P], [LINE, H], [1, w]])).then_inc(toep, 16)
                done += table_blocks(w)
            with sp.Fori(0, IT) as it:
                sp.dma_start(C[0:LK, :, :], ctxt[bass.ds(it * G, G)].rearrange("b k d -> k b d")).then_inc(c_loaded, 16)
                sp.dma_start(X[:], x[bass.ds(it * G, G)].rearrange("b (t p) d -> p (b t) d", p=P)).then_inc(x_loaded, 16)
                for j in range(2):
                    wait(sp, dve_gp, ("f2d", j), it)
                    settle(sp)
                    sp.dma_start(out[bass.ds(it * G + j, 1)].rearrange("b (t p) d -> p (b t) d", p=P),
                                 X[:, 2 * j:2 * j + 2, :]).then_inc(stored, 16)
                sp.wait_ge(stored, it * 32 + 32)
                settle(sp)

        @block.tensor
        def _(pe):
            mm, tr = nc.tensor.matmul, nc.tensor.transpose
            pe.wait_ge(w_loaded, 80)
            pe.wait_ge(ident_made, 4)
            pe.wait_ge(made, 4)
            pe.wait_ge(zeroed, 3)
            pe.wait_ge(flip_made, 2)
            n_block = 0
            for j, (a, tab, w, _) in enumerate(tables):
                pe.wait_ge(toep, 16 * (7 + j))
                nh = H // table_blocks(w)
                for q in range(table_blocks(w)):
                    n_block += 1
                    if n_block > 2:
                        pe.wait_ge(flip_out, n_block - 2)
                    mm(GP[:, n_block % 2, 0:nh * w], flip, staging[:, nh * w * q:nh * w * (q + 1)],
                       start=True, stop=True).then_inc(flip_full, 1)
            pe.wait_ge(flip_out, N_FLIP)
            with pe.Fori(0, IT) as it:
                def take(label):
                    i = use_of[label]
                    if i >= 2:
                        lab, eng = uses[i - 2]
                        wait(pe, act_gp if eng == "act" else dve_gp, lab, it)
                    return bank(label)

                def full(ins):
                    ins.then_inc(gp_full["sem"], 1)

                def enc_transposes(label, src):
                    b_ = take(label)
                    for c in range(KC):
                        for b in range(G):
                            i = tr(b_[:, NE * c + LK * b:NE * c + LK * (b + 1)], src[0:LK, b, P * c:P * (c + 1)],
                                   ident[0:LK, 0:LK])
                    full(i)

                def dec_transposes(name, src, c):
                    b_ = take((*name, c))
                    for t in range(TD):
                        i = tr(b_[:, P * t:P * (t + 1)], src[:, t, P * c:P * (c + 1)], ident[:])
                    full(i)

                def attention(a):
                    src_q = ET if a == ENC else DT
                    src_k = {ENC: ET, XA: CT, SA: DT, CA: ET}[a]
                    nq = NE if a == ENC else ND
                    wq, wk, wv = (w_sb[:, 4 * a + j] for j in range(3))
                    for c in range(KC):
                        if a != ENC or c == 0:
                            b_ = take(("q", a, c))
                        o = b_[:, NE * c:NE * (c + 1)] if a == ENC else b_
                        for k in range(KC):
                            i = mm(o, wq[:, k, P * c:P * (c + 1)], src_q[:, k, 0:nq], start=k == 0, stop=k == KC - 1)
                        if a != ENC or c == 1:
                            full(i)
                    for j in range(2 if a == SA else 1):
                        b_ = take(("v", a, j))
                        for s in range(2):
                            n_k = P if a == SA else LK
                            at = P * (2 * j + s) if a == SA else LK * s
                            for k in range(KC):
                                i = mm(b_[0:n_k, D * s:D * (s + 1)], src_k[:, k, at:at + n_k], wv[:, k, :],
                                       start=k == 0, stop=k == KC - 1)
                        full(i)
                    for s in steps(a):
                        if s[0] == "k":
                            b_ = take(s)
                            n_k, at = (LQ, LQ * (s[1] % 2)) if a == SA else (NE, 0)
                            for c in range(KC):
                                for k in range(KC):
                                    i = mm(b_[:, n_k * c:n_k * (c + 1)], wk[:, k, P * c:P * (c + 1)],
                                           src_k[:, k, at:at + n_k], start=k == 0, stop=k == KC - 1)
                            full(i)
                        elif s[0] == "mx":
                            maxima(a, s[1])
                        elif s[0] == "mt":
                            turn_maxima(a, s)
                        elif s[0] == "st":
                            scores(a, s[1], s[2])
                        elif s[0] == "pv":
                            values(a, s[1], s[2])
                        elif s[0] == "tq":
                            turn_out(a, s)
                        elif s[0] == "tc":
                            turn_back(a, s)

                def maxima(a, n):
                    b, k_step = n % 2, ("k", n) if a == SA else ("k", a)
                    q_at = queries(a) * b
                    k_at = 0 if a == SA else LK * b
                    for i, (t, g, v, nh, nk) in enumerate(max_tiles(a)):
                        c, r = divmod(g, 2)
                        rows_ = slice(64 * r, 64 * r + 64)
                        nt = LK if a == ENC else P
                        wait(pe, qr_ready, (a, c), it)
                        wait(pe, kr_ready, (k_step, c), it)
                        g_i = mx_list.index((n, i))
                        if g_i >= 2:
                            wait(pe, mx_done, mx_list[g_i - 2], it)
                        o = MX[0:nt, i % 2, 0:nh * nk].rearrange("p (h k) -> p h k", h=nh)
                        if a != XA:
                            h0, j0 = 4 * g + v, 0 if a == ENC else P - P * t
                            mm(o, identb[0:nt, 0:nt], tq[a][0:nt, h0:h0 + nh, j0:j0 + nk], start=True, stop=False)
                        ins = mm(o, QR[rows_, c, q_at + P * t:q_at + P * t + nt],
                                 KR[rows_, c, v:v + nh, k_at:k_at + nk], start=a == XA, stop=True)
                        ins.then_inc(mx_full["sem"], 1)

                def turn_maxima(a, s):
                    n = s[1]
                    b_ = take(s)
                    wait(pe, mx_done, (n, len(max_tiles(a)) - 1), it)
                    nt = LK if a == ENC else P
                    for t in range(1 if a == ENC else TQ):
                        i = tr(b_[:, P * t:P * t + nt], NM[0:nt, n % 2, t, :], ident[0:nt, 0:nt])
                    full(i)

                def scores(a, n, u):
                    g, v0, nh, s, q0, nq = units(a)[u]
                    c, r = divmod(g, 2)
                    rows_ = slice(64 * r, 64 * r + 64)
                    b, i = n % 2, unit_of[(n, u)]
                    nk = P if a == SA else LK
                    k_at = P * s if a == SA else LK * b
                    q_at = queries(a) * b + q0
                    if u == 0:
                        wait(pe, act_gp, ("mt", n), it)
                        wait(pe, act_gp, ("q", a, 0 if a == ENC else KC - 1), it)
                    if i >= 2:
                        if unit_list[i - 2][0] // 2 == XA:
                            wait(pe, p_ready, unit_list[i - 2], it)
                        else:
                            wait(pe, st_biased, unit_list[i - 2], it)
                    for j in range(nh):
                        o = ST[0:nk, i % 2, nq * j:nq * (j + 1)]
                        mm(o, pick[rows_, 4 * c + v0 + j, 0:nk], MT[rows_, b, q0:q0 + nq], start=True, stop=False)
                        ins = mm(o, KM[rows_, c, v0 + j, k_at:k_at + nk], QT[rows_, c, q_at:q_at + nq],
                                 start=False, stop=True)
                    ins.then_inc(st_full["sem"], 1)

                def values(a, n, p):
                    us = [(u, x) for u, x in enumerate(units(a)) if x[0] // 2 == p]
                    wait(pe, p_ready, (n, us[-1][0]), it)
                    if p == 0:
                        wait(pe, dve_gp, ("v", a, n % 2 if a == SA else 0), it)
                    if n > 0:
                        wait(pe, oc_ready, (n - 1, p), it)
                    for g in (2 * p, 2 * p + 1):
                        for s in range(2 if a == SA else 1):
                            for v in range(4):
                                u, (_, v0, nh, _, q0, nq) = next(
                                    (u, x) for u, x in us if x[0] == g and x[3] == s and x[1] <= v < x[1] + x[2])
                                slot = unit_of[(n, u)] % 8
                                nk = P if a == SA else LK
                                vs = 2 * (n % 2) + s if a == SA else n % 2
                                ins = mm(OT[32 * v:32 * v + HD + 1, g, q0:q0 + nq], V[0:nk, vs, 4 * g + v, :],
                                         PR[0:nk, slot, nq * (v - v0):nq * (v - v0 + 1)],
                                         start=s == 0, stop=s == (1 if a == SA else 0), tile_position=(0, 32 * v))
                    ins.then_inc(pv_done["sem"], 1)

                def turn_out(a, s):
                    _, n, t = s
                    b_ = take(s)
                    wait(pe, oc_ready, (n, 1), it)
                    nt = LK if a == ENC else P
                    for g in range(4):
                        i = tr(b_[0:nt, P * g:P * (g + 1)], OC[:, g, P * t:P * t + nt], ident[:])
                    full(i)

                def turn_back(a, s):
                    n = s[1]
                    qt = 1 if a == ENC else TQ
                    b_ = take(s)
                    wait(pe, dve_gp, ("tq", n, qt - 1), it)
                    nt = LK if a == ENC else P
                    for c in range(KC):
                        for t in range(qt):
                            i = tr(b_[:, LQ * c + P * t:LQ * c + P * t + nt], CN[0:nt, t, P * c:P * (c + 1)],
                                   ident[0:nt, 0:nt])
                    full(i)

                def out_projection(a):
                    wo = w_sb[:, 4 * a + 3]
                    src, nt = (ET, LK) if a == ENC else (DT, P)
                    for j in range(1 if a == ENC else 2):
                        b_ = take(("o", a, j))
                        wait(pe, act_gp, ("tc", 2 * a + (1 if a == ENC else j)), it)
                        for s in range(2):
                            at = nt * (2 * j + s)
                            for k in range(KC):
                                i = mm(b_[0:nt, D * s:D * (s + 1)], src[:, k, at:at + nt], wo[:, k, :],
                                       start=k == 0, stop=k == KC - 1)
                        full(i)

                def hidden(e, label, src, o_cols, m):
                    for j in range(len(m)):
                        for k in range(KC):
                            i = mm(o_cols[j], ff1_sb[:, e, k, P * m[j]:P * (m[j] + 1)], src[k],
                                   start=k == 0, stop=k == KC - 1)
                    full(i)

                pe.wait_ge(c_loaded, it * 16 + 16)
                enc_transposes("ct", C)
                wait(pe, xn_ready, ("E1", G - 1), it)
                enc_transposes("et", XE)
                pe.wait_ge(x_loaded, it * 16 + 16)
                for c in range(KC):
                    dec_transposes(("xt",), X, c)
                wait(pe, act_gp, "et", it)
                attention(ENC)
                out_projection(ENC)
                wait(pe, act_gp, ("xt", 1), it)
                attention(XA)
                out_projection(XA)
                wait(pe, xn_ready, ("E2", G - 1), it)
                enc_transposes("ht", XE)
                wait(pe, act_gp, "ht", it)
                for j in range(FC // 2):
                    b_ = take(("f1e", j))
                    hidden(0, ("f1e", j), [ET[:, k, :] for k in range(KC)], [b_[:, NE * s:NE * (s + 1)] for s in range(2)],
                           [2 * j, 2 * j + 1])
                b_ = take("f2e")
                wait(pe, act_gp, ("f1e", FC // 2 - 1), it)
                for b in range(G):
                    for m in range(FC):
                        i = mm(b_[0:LK, D * b:D * (b + 1)], HID[:, m, LK * b:LK * (b + 1)], ff2_sb[:, 0, m, :],
                               start=m == 0, stop=m == FC - 1)
                full(i)
                wait(pe, dve_gp, "f2e", it)
                enc_transposes("mem", C)
                for a, l in ((SA, "D1"), (CA, "D2")):
                    wait(pe, xn_ready, (l, TD - 1), it)
                    for c in range(KC):
                        dec_transposes(("yt", a), XN, c)
                    wait(pe, act_gp, ("yt", a, 1), it)
                    attention(a)
                    out_projection(a)
                wait(pe, xn_ready, ("D3", TD - 1), it)
                for c in range(KC):
                    dec_transposes(("yt", "ff"), XN, c)
                wait(pe, act_gp, ("yt", "ff", 1), it)
                for j in range(FC):
                    b_ = take(("f1d", j))
                    hidden(1, ("f1d", j), [DT[:, k, :] for k in range(KC)], [b_], [j])
                wait(pe, act_gp, ("f1d", FC - 1), it)
                for j in range(2):
                    b_ = take(("f2d", j))
                    for s in range(2):
                        for m in range(FC):
                            i = mm(b_[:, D * s:D * (s + 1)], HID[:, m, P * (2 * j + s):P * (2 * j + s + 1)],
                                   ff2_sb[:, 1, m, :], start=m == 0, stop=m == FC - 1)
                    full(i)

        @block.scalar
        def _(act):
            copy = nc.scalar.copy
            n_block = 0
            for a, tab, w, _ in tables:
                nh = H // table_blocks(w)
                for q in range(table_blocks(w)):
                    n_block += 1
                    act.wait_ge(flip_full, n_block)
                    copy(tab[:, nh * q:nh * (q + 1), :],
                         GP[:, n_block % 2, 0:nh * w].rearrange("p (h w) -> p h w", h=nh)).then_inc(flip_out, 1)
            act.wait_ge(w_loaded, 80)
            with act.Fori(0, IT) as it:
                def emptied(ins):
                    ins.then_inc(act_gp["sem"], 1)

                def filled(label):
                    wait(act, gp_full, label, it)
                    return bank(label)

                def enc_features(label, dst, scale=None, bias=None):
                    b_ = filled(label)
                    if scale is None:
                        i = copy(dst[:].rearrange("p c n -> p (c n)"), b_[:, 0:KC * NE])
                    else:
                        for c in range(KC):
                            i = nc.scalar.activation(dst[:, c, :], b_[:, NE * c:NE * (c + 1)], ACT.Identity,
                                                     bias=col(bias, c), scale=col(scale, c))
                    emptied(i)

                def dec_features(name, dst, scale=None, bias=None):
                    for c in range(KC):
                        b_ = filled((*name, c))
                        if scale is None:
                            emptied(copy(dst[:, c, :], b_))
                        else:
                            emptied(nc.scalar.activation(dst[:, c, :], b_, ACT.Identity,
                                                         bias=col(bias, c), scale=col(scale, c)))

                def attention(a):
                    if a > 0:
                        wait(act, st_full, (2 * a - 1, len(units(a - 1)) - 1), it)
                    for c in range(KC):
                        b_ = filled(("q", a, 0 if a == ENC else c))
                        src = b_[:, NE * c:NE * (c + 1)] if a == ENC else b_
                        i = nc.scalar.activation(QT[:, c, 0:NE if a == ENC else ND], src, ACT.Identity,
                                                 bias=col(PRE[a] + "_bq", c), scale=1.0)
                        if a != ENC or c == 1:
                            emptied(i)
                    for s in steps(a):
                        if s[0] == "mt":
                            n = s[1]
                            b_ = filled(s)
                            if n >= 2:
                                wait(act, st_full, (n - 2, len(units((n - 2) // 2)) - 1), it)
                            nt = queries(a)
                            emptied(copy(MT[:, n % 2, 0:nt], b_[:, 0:nt]))
                        elif s[0] == "st":
                            n, u = s[1], s[2]
                            i = unit_of[(n, u)]
                            nk = P if a == SA else LK
                            w = units(a)[u][2] * units(a)[u][5]
                            if a == XA:
                                wait(act, st_full, (n, u), it)
                                if last_reader(i):
                                    wait(act, pv_done, last_reader(i), it)
                                src = ST[0:nk, i % 2, 0:w]
                            else:
                                wait(act, st_biased, (n, u), it)
                                src = PR[0:nk, i % 8, 0:w]
                            nc.scalar.activation(PR[0:nk, i % 8, 0:w], src, ACT.Exp).then_inc(p_ready["sem"], 1)
                        elif s[0] == "pv":
                            n, p = s[1], s[2]
                            wait(act, pv_done, (n, p), it)
                            if n % 2 == 1 and p == 0:
                                wait(act, gp_full, ("tq", n - 1, (1 if a == ENC else TQ) - 1), it)
                            if n == 2 * a and p == 0 and a > 0:
                                wait(act, gp_full, ("tq", n - 1, (1 if a == XA else TQ) - 1), it)
                            nq = queries(a)
                            copy(OC[:, 2 * p:2 * p + 2, 0:nq], OT[:, 2 * p:2 * p + 2, 0:nq]).then_inc(oc_ready["sem"], 1)
                        elif s[0] == "tc":
                            n = s[1]
                            b_ = filled(s)
                            nt = queries(a)
                            dst = (ET if a == ENC else DT)[:, :, nt * (n % 2):nt * (n % 2 + 1)]
                            emptied(copy(dst, b_.rearrange("p (c n) -> p c n", c=KC)[:, :, 0:nt]))

                enc_features("ct", CT)
                enc_features("et", ET, "enc_n1_s", "enc_n1_b")
                dec_features(("xt",), DT)
                attention(ENC)
                attention(XA)
                enc_features("ht", ET, "enc_n2_s", "enc_n2_b")
                wait(act, pv_done, (3, 1), it)
                for j in range(FC // 2):
                    b_ = filled(("f1e", j))
                    for s in range(2):
                        i = nc.scalar.activation(HID[:, 2 * j + s, 0:NE], b_[:, NE * s:NE * (s + 1)], ACT.Relu,
                                                 bias=col("enc_ff1", 2 * j + s), scale=1.0)
                    emptied(i)
                enc_features("mem", ET)
                dec_features(("yt", SA), DT, "dec_n1_s", "dec_n1_b")
                attention(SA)
                dec_features(("yt", CA), DT, "dec_n2_s", "dec_n2_b")
                attention(CA)
                dec_features(("yt", "ff"), DT, "dec_n3_s", "dec_n3_b")
                for j in range(FC):
                    b_ = filled(("f1d", j))
                    emptied(nc.scalar.activation(HID[:, j, :], b_, ACT.Relu, bias=col("dec_ff1", j), scale=1.0))

        @block.vector
        def _(dve):
            tt, ts, cp = nc.vector.tensor_tensor, nc.vector.tensor_scalar, nc.vector.tensor_copy
            nc.vector.memset(NM[:], 0.0).then_inc(zeroed, 1)
            nc.vector.memset(V[:], 1.0).then_inc(zeroed, 1)
            nc.vector.memset(OT[:], 0.0).then_inc(zeroed, 1)
            dve.wait_ge(toep, 96)
            for r in range(3):
                up, down = rel_sb[:, r, 0, :], rel_sb[:, r, 1, :]
                lk_, lq_ = line(2 * r), line(2 * r + 1)
                far = up[:, P - 1:P]
                if REL[r] == SA:
                    cp(lk_[:, P - 1:P], down[:, P - 1:P])
                    nc.vector.memset(lk_[:, 0:P - 1], MASKED)
                else:
                    cp(lk_[:, 0:P], down[:, 0:P])
                cp(lk_[:, P:2 * P - 1], up[:, 1:P])
                cp(lk_[:, 2 * P - 1:LINE], far.broadcast_to([H, LINE - 2 * P + 1])).then_inc(built, 1)
                cp(lq_[:, 0:P], far.broadcast_to([H, P]))
                cp(lq_[:, P:2 * P - 1], down[:, P:2 * P - 1])
                if REL[r] == SA:
                    nc.vector.memset(lq_[:, 2 * P:LINE], MASKED)
                    cp(lq_[:, 2 * P - 1:2 * P], up[:, P:P + 1]).then_inc(built, 1)
                else:
                    nc.vector.memset(lq_[:, LINE - 1:LINE], 0.0)
                    cp(lq_[:, 2 * P - 1:LINE - 1], up[:, P:2 * P]).then_inc(built, 1)
            dve.wait_ge(ident_made, 3)
            cp(identb[:], ident[:]).then_inc(ident_made, 1)
            dve.wait_ge(ident_made, 4)
            cp(pick[0:64], identb[0:64, 0:8].rearrange("p (i o) -> p i o", o=1).broadcast_to([64, 8, P])).then_inc(made, 1)
            cp(pick[64:P], identb[64:P, 64:72].rearrange("p (i o) -> p i o", o=1).broadcast_to([64, 8, P])).then_inc(made, 1)
            nc.vector.tensor_reduce(head_mask[:], ident[:].rearrange("p (r v d) -> p v r d", r=2, v=4), AX.XY,
                                    ALU.add).then_inc(made, 1)
            dve.wait_ge(made, 3)
            ts(head_mask[:], head_mask[:], SCALE, None, ALU.mult).then_inc(made, 1)
            dve.wait_ge(made, 4)
            dve.wait_ge(w_loaded, 80)
            dve.wait_ge(flip_out, N_FLIP)
            dve.wait_ge(zeroed, 3)
            with dve.Fori(0, IT) as it:
                def emptied(ins):
                    ins.then_inc(dve_gp["sem"], 1)

                def filled(label):
                    wait(dve, gp_full, label, it)
                    return bank(label)

                def normalise(l, src, dst, np_):
                    for t in range(ln_tiles[l]):
                        nc.vector.bn_stats(st6[0:np_, t, :], src[0:np_, t, :]).then_inc(stats["sem"], 1)
                    wait(dve, stats, (l, ln_tiles[l] - 1), it)
                    settle(dve)
                    for t in range(ln_tiles[l]):
                        nc.vector.bn_aggr(mv[0:np_, t, :], st6[0:np_, t, :]).then_inc(aggr["sem"], 1)
                    wait(dve, rstd_ready, l, it)
                    for t in range(ln_tiles[l]):
                        ts(dst[0:np_, t, :], src[0:np_, t, :], mv[0:np_, t, 0:1], rstd[0:np_, t:t + 1],
                           ALU.subtract, ALU.mult).then_inc(xn_ready["sem"], 1)

                def attention(a):
                    nk = P if a == SA else LK
                    if a > 0:
                        wait(dve, pv_done, (2 * a - 1, 1), it)
                    for j in range(2 if a == SA else 1):
                        b_ = filled(("v", a, j))
                        bv = row_sb[0:nk, ROW[PRE[a] + "_bv"], :].rearrange("p (h d) -> p h d", h=H)
                        for s in range(2):
                            i = tt(V[0:nk, 2 * j + s, :, 0:HD], b_[0:nk, D * s:D * (s + 1)].rearrange("p (h d) -> p h d", h=H),
                                   bv, ALU.add)
                        emptied(i)
                    for s in steps(a):
                        if s[0] == "k":
                            b_ = filled(s)
                            w = LQ if a == SA else NE
                            last = s[1] - 1 if a == SA else 2 * a - 1
                            if last >= 0:
                                wait(dve, st_full, (last, len(units(last // 2)) - 1), it)
                            for c in range(KC):
                                for v in range(4):
                                    i = ts(KM[:, c, v, 0:w], b_[:, w * c:w * (c + 1)], col(PRE[a] + "_bk", c),
                                           head_mask[:, v:v + 1], ALU.add, ALU.mult)
                            emptied(i)
                        elif s[0] == "mx":
                            n = s[1]
                            for i, (t, g, v, nh, n_keys) in enumerate(max_tiles(a)):
                                c, r = divmod(g, 2)
                                nt = LK if a == ENC else P
                                wait(dve, mx_full, (n, i), it)
                                nc.vector.tensor_reduce(
                                    NM[0:nt, n % 2, t, 64 * r + 4 * c + v:64 * r + 4 * c + v + nh],
                                    MX[0:nt, i % 2, 0:nh * n_keys].rearrange("p (h k) -> p h k", h=nh),
                                    AX.X, ALU.max, negate=True).then_inc(mx_done["sem"], 1)
                        elif s[0] == "st" and a != XA:
                            n, u = s[1], s[2]
                            g, v0, nh, ks, q0, nq = units(a)[u]
                            i = unit_of[(n, u)]
                            wait(dve, st_full, (n, u), it)
                            if last_reader(i):
                                wait(dve, pv_done, last_reader(i), it)
                            h0 = 4 * g + v0
                            tt(PR[0:nk, i % 8, 0:nh * nq].rearrange("p (h q) -> p h q", h=nh),
                               ST[0:nk, i % 2, 0:nh * nq].rearrange("p (h q) -> p h q", h=nh),
                               tk[a][0:nk, h0:h0 + nh, 0:nq], ALU.add).then_inc(st_biased["sem"], 1)
                        elif s[0] == "tq":
                            _, n, t = s
                            nt = LK if a == ENC else P
                            b_ = filled(s)
                            if n % 2 == 1 and t == 0:
                                wait(dve, gp_full, ("tc", n - 1), it)
                            o = b_[0:nt, :].rearrange("p (h d) -> p h d", d=32)
                            i_tq = tq_list.index(s)
                            rd = rden[0:nt, i_tq % 2, :].rearrange("p (h o) -> p h o", o=1)
                            if i_tq >= 2:
                                wait(dve, dve_gp, tq_list[i_tq - 2], it)
                            nc.vector.reciprocal(rd,
                                                 o[:, :, HD:HD + 1]).then_inc(den_ready["sem"], 1)
                            wait(dve, den_ready, s, it)
                            emptied(tt(CN[0:nt, t, :].rearrange("p (h d) -> p h d", h=H), o[:, :, 0:HD],
                                       rd.broadcast_to([nt, H, HD]),
                                       ALU.mult))

                def add_to_stream(label, dst):
                    b_ = filled(label)
                    np_ = dst.shape[0]
                    return tt(dst, b_[0:np_, :].rearrange("p (t d) -> p t d", t=2), dst, ALU.add)

                dve.wait_ge(c_loaded, it * 16 + 16)
                normalise("E1", C, XE, LK)
                attention(ENC)
                wait(dve, pre_added, "enc_bo", it)
                emptied(add_to_stream(("o", ENC, 0), C[0:LK, :, :]))
                wait(dve, dve_gp, ("o", ENC, 0), it)
                normalise("E2", C, XE, LK)
                attention(XA)
                wait(dve, pre_added, "xa_bo", it)
                for j in range(2):
                    emptied(add_to_stream(("o", XA, j), X[:, 2 * j:2 * j + 2, :]))
                wait(dve, dve_gp, ("o", XA, 1), it)
                normalise("L0", X, XN, P)
                wait(dve, xn_ready, ("L0", TD - 1), it)
                gam = row_sb[:, ROW["gamma"]:ROW["gamma"] + 1, :].broadcast_to([P, TD, D])
                bet = row_sb[:, ROW["beta"]:ROW["beta"] + 1, :].broadcast_to([P, TD, D])
                tt(XN[:], XN[:], gam, ALU.mult).then_inc(l0_affine["sem"], 1)
                wait(dve, l0_affine, "gamma", it)
                tt(X[:], XN[:], bet, ALU.add).then_inc(l0_affine["sem"], 1)
                wait(dve, l0_affine, "beta", it)
                normalise("D1", X, XN, P)
                wait(dve, pre_added, "enc_ff2", it)
                emptied(add_to_stream("f2e", C[0:LK, :, :]))
                for a, l in ((SA, "D2"), (CA, "D3")):
                    attention(a)
                    wait(dve, pre_added, PRE[a] + "_bo", it)
                    for j in range(2):
                        emptied(add_to_stream(("o", a, j), X[:, 2 * j:2 * j + 2, :]))
                    wait(dve, dve_gp, ("o", a, 1), it)
                    normalise(l, X, XN, P)
                wait(dve, pre_added, "dec_ff2", it)
                for j in range(2):
                    emptied(add_to_stream(("f2d", j), X[:, 2 * j:2 * j + 2, :]))

        @block.gpsimd
        def _(pool):
            nc.gpsimd.memset(ident[:], 0.0).then_inc(ident_made, 1)
            pool.wait_ge(ident_made, 1)
            nc.gpsimd.affine_select(out=ident[:], in_=ident[:], compare_op=ALU.not_equal, fill=1.0, base=0,
                                    pattern=[[-1, P]], channel_multiplier=1).then_inc(ident_made, 1)
            nc.gpsimd.memset(exponent[:], -0.5).then_inc(ident_made, 1)
            nc.gpsimd.memset(flip, 0.0).then_inc(flip_made, 1)
            pool.wait_ge(flip_made, 1)
            nc.gpsimd.affine_select(out=flip, in_=flip, compare_op=ALU.not_equal, fill=1.0, base=1 - P,
                                    pattern=[[1, P]], channel_multiplier=1).then_inc(flip_made, 1)
            pool.wait_ge(ident_made, 3)
            pool.wait_ge(w_loaded, 80)
            with pool.Fori(0, IT) as it:
                def inverse_deviation(l, np_):
                    n_t = ln_tiles[l]
                    eps = EPS_L0 if l == "L0" else EPS_L1
                    wait(pool, aggr, (l, n_t - 1), it)
                    settle(pool)
                    nc.gpsimd.tensor_scalar(ve[0:np_, 0:n_t], mv[0:np_, 0:n_t, 1], eps, 1.0, ALU.add,
                                            ALU.mult).then_inc(eps_added["sem"], 1)
                    wait(pool, eps_added, l, it)
                    nc.gpsimd.tensor_tensor(rstd[0:np_, 0:n_t], ve[0:np_, 0:n_t], exponent[0:np_, 0:n_t],
                                            ALU.pow).then_inc(rstd_ready["sem"], 1)

                def add_row(name, dst):
                    np_, n_t, _ = dst.shape
                    r = row_sb[0:np_, ROW[name]:ROW[name] + 1, :].broadcast_to([np_, n_t, D])
                    nc.gpsimd.tensor_tensor(dst, dst, r, ALU.add).then_inc(pre_added["sem"], 1)

                def attention(a):
                    w = NE if a == ENC else ND
                    if a > 0:
                        wait(pool, mx_full, (2 * a - 1, len(max_tiles(a - 1)) - 1), it)
                    for c in range(KC):
                        wait(pool, act_gp, ("q", a, 0 if a == ENC else c), it)
                        settle(pool)
                        nc.gpsimd.tensor_copy(QR[:, c, 0:w], QT[:, c, 0:w]).then_inc(qr_ready["sem"], 1)
                    for s in steps(a):
                        if s[0] == "k":
                            wait(pool, dve_gp, s, it)
                            if a == SA and s[1] % 2:
                                wait(pool, mx_full, (s[1] - 1, len(max_tiles(a)) - 1), it)
                            settle(pool)
                            w = LQ if a == SA else NE
                            for c in range(KC):
                                nc.gpsimd.tensor_copy(KR[:, c, :, 0:w], KM[:, c, :, 0:w]).then_inc(kr_ready["sem"], 1)

                inverse_deviation("E1", LK)
                wait(pool, gp_full, "ct", it)
                wait(pool, xn_ready, ("E1", G - 1), it)
                add_row("enc_bo", C[0:LK, :, :])
                wait(pool, gp_full, ("xt", 1), it)
                add_row("xa_bo", X[:])
                attention(ENC)
                inverse_deviation("E2", LK)
                wait(pool, xn_ready, ("E2", G - 1), it)
                add_row("enc_ff2", C[0:LK, :, :])
                attention(XA)
                inverse_deviation("L0", P)
                inverse_deviation("D1", P)
                wait(pool, xn_ready, ("D1", TD - 1), it)
                add_row("sa_bo", X[:])
                attention(SA)
                inverse_deviation("D2", P)
                wait(pool, xn_ready, ("D2", TD - 1), it)
                add_row("ca_bo", X[:])
                attention(CA)
                inverse_deviation("D3", P)
                wait(pool, xn_ready, ("D3", TD - 1), it)
                add_row("dec_ff2", X[:])


_ATT = ["enc", "xa", "sa", "ca"]


def kernel(**inputs):
    import numpy as _np
    import concourse.bacc as _bacc
    from concourse import mybir as _mybir
    from concourse.bass_utils import run_bass_kernel_spmd as _run

    i = {k: _np.asarray(v) for k, v in inputs.items()}
    l0 = lambda k: i["L0_xattn_" + k]
    l1 = lambda k: i["L1_xattn_" + k]
    in_w = [l1("enc_in_w"), None, l1("dec_sa_in_w"), l1("dec_ca_in_w")]
    out_w = [l1("enc_out_w"), None, l1("dec_sa_out_w"), l1("dec_ca_out_w")]
    in_b = [l1("enc_in_b"), _np.concatenate([l0("bq"), l0("bk"), l0("bv")]), l1("dec_sa_in_b"), l1("dec_ca_in_b")]
    out_b = [l1("enc_out_b"), l0("bo"), l1("dec_sa_out_b"), l1("dec_ca_out_b")]
    mats = []
    for a in range(4):
        if in_w[a] is None:
            mats += [l0("Wq"), l0("Wk"), l0("Wv"), l0("Wo")]
        else:
            mats += [in_w[a][D * j:D * (j + 1)].T for j in range(3)] + [out_w[a].T]

    def chunks(m):
        return m.reshape(-1, P, m.shape[1]).transpose(1, 0, 2).reshape(P, -1)

    wm = _np.stack([chunks(m) for m in mats], 1)
    wff1 = _np.stack([chunks(l1("enc_ff1_w").T), chunks(l1("dec_ff1_w").T)], 1)
    wff2 = _np.stack([chunks(l1("enc_ff2_w").T), chunks(l1("dec_ff2_w").T)], 1)
    vecs = {}
    for a, p in enumerate(_ATT):
        vecs[p + "_bq"], vecs[p + "_bk"], vecs[p + "_bv"] = (in_b[a][D * j:D * (j + 1)] for j in range(3))
        vecs[p + "_bo"] = out_b[a]
    for k in ("enc_n1", "enc_n2", "dec_n1", "dec_n2", "dec_n3"):
        vecs[k + "_s"], vecs[k + "_b"] = l1(k + "_s"), l1(k + "_b")
    vecs["gamma"], vecs["beta"] = l0("ln_gamma"), l0("ln_beta")
    vecs["enc_ff2"], vecs["dec_ff2"] = l1("enc_ff2_b"), l1("dec_ff2_b")
    cols = _np.concatenate([vecs[k].reshape(-1, P).T for k in COLS]
                           + [l1("enc_ff1_b").reshape(-1, P).T, l1("dec_ff1_b").reshape(-1, P).T], 1)
    rows = _np.stack([vecs[k] for k in ROWS])
    rels = [l1("enc_rel"), l1("dec_rel_self"), l1("dec_rel_cross")]
    arrays = {"x": i["x"], "ctxt": i["ctx_1024"], "wm": wm, "wff1": wff1, "wff2": wff2, "cols": cols, "rows": rows,
              "rel_up": _np.stack([r.T for r in rels]), "rel_down": _np.stack([r[::-1].T for r in rels])}
    nc = _bacc.Bacc("TRN2", target_bir_lowering=False, num_devices=1)
    feed, args = {}, []
    for name, a in arrays.items():
        a = _np.ascontiguousarray(a)
        feed[f"in_{name}"] = a
        args.append(nc.dram_tensor(f"in_{name}", a.shape, _mybir.dt.from_np(a.dtype), kind="ExternalInput").ap())
    args.append(nc.dram_tensor("out_0", (NB, LQ, D), _mybir.dt.float32, kind="ExternalOutput").ap())
    build(nc, *args)
    r = _run(nc, [feed], core_ids=[0])
    return r.results[0]["out_0"]
```

```python
from contextlib import ExitStack

import concourse.bass as bass
from concourse import mybir

F32 = mybir.dt.float32
BF16 = mybir.dt.bfloat16
ALU = mybir.AluOpType
ACT = mybir.ActivationFunctionType
AX = mybir.AxisListType

NB, LQ, D = 64, 256, 256
LK = 120
H, HD = 16, 16
DFF = 1024
P = 128
KC = D // P
TQ = LQ // P
FC = DFF // P
SCALE = 1.0 / HD ** 0.5
MASKED = -1.0e30
EPS_L0, EPS_L1 = 1e-5, 1e-6
ENC, XA, SA, CA = range(4)

COLS = ["enc_bq", "enc_bk", "xa_bq", "xa_bk", "sa_bq", "sa_bk", "ca_bq", "ca_bk",
        "enc_bv", "xa_bv", "sa_bv", "ca_bv",
        "enc_n1_s", "enc_n1_b", "enc_n2_s", "enc_n2_b",
        "dec_n1_s", "dec_n1_b", "dec_n2_s", "dec_n2_b", "dec_n3_s", "dec_n3_b"]
COL = {name: KC * i for i, name in enumerate(COLS)}
COL["enc_ff1"] = KC * len(COLS)
COL["dec_ff1"] = COL["enc_ff1"] + FC
NCOL = COL["dec_ff1"] + FC
ROWS = ["enc_bo", "xa_bo", "sa_bo", "ca_bo", "enc_ff2", "dec_ff2", "gamma", "beta"]
ROW = {name: i for i, name in enumerate(ROWS)}
PRE = ["enc", "xa", "sa", "ca"]
LINE = 384


def queries(a):
    return LK if a == ENC else LQ


def key_tile(a):
    return P if a == SA else LK


def keys(a):
    return LQ if a == SA else LK


def query_tiles(a):
    return 1 if a == ENC else TQ


def chain_of(a):
    return "A" if a in (ENC, XA) else "B"


def units(a):
    if a == ENC:
        return [(g, 0, 4, 0, 0, LK) for g in range(4)]
    return [x for g in range(4) for x in [(g, 0, 2, 0, 0, LQ), (g, 2, 2, 0, 0, LQ)]
            + [(g, 0, 4, 1, P, LQ - P)] * (a == SA)]


def max_tiles(a):
    if a == ENC:
        return [(0, g, 0, 4, LK) for g in range(4)]
    if a != SA:
        return [(t, g, 0, 4, LK) for t in range(TQ) for g in range(4)]
    return ([(0, g, 0, 4, P) for g in range(4)]
            + [(1, 2 * c + r, v, 2, 2 * P) for c in range(2) for v in (0, 2) for r in range(2)])


def prepare(a, kinds):
    return [(k, a) for k in kinds] + [("mx", a, i) for i in range(len(max_tiles(a)))]


def softmax(a):
    n, out = len(units(a)) // 4, [("mt", a)]
    for u in range(4 * n):
        out.append(("st", a, u))
        if u and u % n == 0:
            out.append(("pv", a, u // n - 1))
    return out + [("pv", a, 3)] + [("tq", a, t) for t in range(query_tiles(a))] + [("tc", a), ("o", a)]


CHAIN_A = ([("ct",), ("ln", "E1"), ("xt",), ("et", ENC)] + prepare(ENC, "qkv") + softmax(ENC) + [("ln", "E2")]
           + [("et", "ff")] + prepare(XA, "qkv") + [("f1", "A", 0), ("f1", "A", 1)] + softmax(XA)[:4]
           + [("f2", "A")] + softmax(XA)[4:] + [("ln", "L0"), ("mem",)])
CHAIN_B = ([("affine",), ("ln", "D1"), ("yt", SA)] + prepare(SA, "qkv") + softmax(SA) + [("ln", "D2")]
           + [("k", CA), ("v", CA), ("yt", CA)] + prepare(CA, "q") + softmax(CA) + [("ln", "D3"), ("yt", "ff")]
           + [("f1", "B", j) for j in range(4)] + [("f2", "B")])


def weight(s):
    k = s[0]
    a = s[1] if len(s) > 1 else None
    enc = a in (ENC, "A")
    return {"ct": .6, "xt": 1.2, "et": 2, "yt": 2.5, "mem": 1, "ln": 5, "affine": 2, "q": 1.2 if enc else 2.4,
            "k": 2.5 if enc else 3, "v": .8 if enc else 1.8, "mx": .7, "mt": 2.5, "st": 1.2, "pv": 1.0 if enc else 1.4,
            "tq": 1.2, "tc": 2, "o": 1.5 if enc else 2.5, "f1": 1.8, "f2": 3}[k]


def merge(a, b):
    out, i, j, ta, tb = [], 0, 0, 0.0, 0.0
    wa, wb = sum(map(weight, a)), sum(map(weight, b))
    while i < len(a) or j < len(b):
        if j == len(b) or (i < len(a) and ta / wa < tb / wb):
            out.append(a[i])
            ta += weight(a[i])
            i += 1
        else:
            out.append(b[j])
            tb += weight(b[j])
            j += 1
    return out


ORDER = merge(CHAIN_A, CHAIN_B)
CHAIN = {s: "A" for s in CHAIN_A} | {s: "B" for s in CHAIN_B}
GENERAL = {"ct": "act", "xt": "act", "et": "act", "yt": "act", "mem": "act", "q": "act", "k": "dve keys", "v": "dve",
           "mt": "act", "tq": "dve", "tc": "act", "o": "dve", "f1": "act", "f2": "dve"}
NBANK = {"gp": 2, "mx": 2, "st": 2, "ot": 2}


def ring(kinds):
    return [s for s in ORDER if s[0] in kinds]


RINGS = {"gp": ring(GENERAL), "mx": ring(["mx"]), "st": ring(["st"]), "ot": ring(["pv"])}
RING_OF = {s: r for r, xs in RINGS.items() for s in xs}
MR = 64 + 8
SLOTS = {"A": 3, "B": 5}
UNITS = {c: [s for s in ORDER if s[0] == "st" and CHAIN[s] == c] for c in "AB"}
assert all(len(UNITS[c]) % SLOTS[c] == 0 for c in "AB")


def before(step, ring_name, size, phase):
    xs = RINGS[ring_name]
    at = xs.index(step)
    for i in range(at - 1, -1, -1):
        if i % size == at % size and CHAIN[xs[i]] in phase:
            return xs[i], True
    was = {"A": "", "AB": "AB", "B": "AB"}[phase]
    for i in range(len(xs) - 1, -1, -1):
        if i % size == at % size and CHAIN[xs[i]] in was:
            return xs[i], False
    return None, False


def unit_slot(a, u):
    c = chain_of(a)
    return 3 * (c == "B") + UNITS[c].index(("st", a, u)) % SLOTS[c]


def value_step(a, u):
    return ("pv", a, 4 * u // len(units(a)))


for c in "AB":
    for was, s in zip(UNITS[c], UNITS[c][SLOTS[c]:]):
        assert ORDER.index(value_step(*was[1:])) < ORDER.index(s), (was, s)
assert ORDER.index(("k", CA)) < ORDER.index(("mem",)) and ORDER.index(("v", CA)) < ORDER.index(("mem",))
assert ORDER[0] == ("affine",) or ORDER[1] == ("affine",)


def build(nc, x, ctxt, wm, wff1, wff2, cols, rows, rel_up, rel_down, out):
    with ExitStack() as stack:
        def sb(name, shape, dt=F32):
            return stack.enter_context(nc.sbuf_tensor(name, shape, dt))

        def ps(name, shape):
            return stack.enter_context(nc.psum_tensor(name, shape, F32))

        def sem(name):
            return stack.enter_context(nc.semaphore(name))

        w_sb = sb("w_sb", [P, 16, KC, D])
        ff1_sb = sb("ff1_sb", [P, 2, KC, DFF])
        ff2_sb = sb("ff2_sb", [P, 2, FC, D])
        col_sb = sb("col_sb", [P, NCOL])
        row_sb = sb("row_sb", [P, len(ROWS), D])
        ident = sb("ident", [P, P])
        identb = sb("identb", [P, P], BF16)
        head_mask = sb("head_mask", [P, 4])
        exponent = sb("exponent", [P, TQ])
        tk = {ENC: sb("tk_enc", [P, H, LK]), SA: sb("tk_sa", [P, H, LQ]), CA: sb("tk_ca", [P, H, LQ])}
        tq = {ENC: sb("tq_enc", [P, H, LK], BF16), SA: sb("tq_sa", [P, H, LQ], BF16), CA: sb("tq_ca", [P, H, LQ], BF16)}
        X = sb("X", [P, TQ, D])
        C = sb("C", [P, 1, D])
        CT = sb("CT", [P, KC, LK])
        ET = sb("ET", [P, KC, LK])
        XT = sb("XT", [P, KC, LQ])
        MEMT = sb("MEMT", [P, KC, LK])
        Y = sb("Y", [P, TQ, D])
        YT = sb("YT", [P, KC, LQ])
        XN = {c: sb("XN" + c, [P, TQ, D]) for c in "AB"}
        CN = XN
        QT = {c: sb("QT" + c, [P, KC, 2, LQ]) for c in "AB"}
        QR = {c: sb("QR" + c, [P, KC, 2, LQ], BF16) for c in "AB"}
        KM = {c: sb("KM" + c, [P, KC, 4, w]) for c, w in (("A", LK), ("B", LQ))}
        KR = {c: sb("KR" + c, [P, KC, 4, w], BF16) for c, w in (("A", LK), ("B", LQ))}
        V = {c: sb("V" + c, [P, n, H, HD + 1]) for c, n in (("A", 1), ("B", 2))}
        OC = {c: sb("OC" + c, [P, 4, LQ]) for c in "AB"}
        XE = OC["A"][:, 0:1, :]
        NM = {c: sb("NM" + c, [P, TQ, MR]) for c in "AB"}
        MT = {c: sb("MT" + c, [P, LQ], BF16) for c in "AB"}
        HID = {"A": OC["A"][:].rearrange("p g n -> p (g n)")[:, 0:FC * LK].rearrange("p (m n) -> p m n", m=FC),
               "B": KM["B"][:].rearrange("p c v n -> p (c v) n")}
        PR = sb("PR", [P, sum(SLOTS.values()), 512])
        st6 = {c: sb("st6" + c, [P, TQ, 6]) for c in "AB"}
        mv = {c: sb("mv" + c, [P, TQ, 2]) for c in "AB"}
        ve = {c: sb("ve" + c, [P, TQ]) for c in "AB"}
        rstd = {c: sb("rstd" + c, [P, TQ]) for c in "AB"}
        rden = {c: sb("rden" + c, [P, 2, H]) for c in "AB"}
        PS = {"gp": ps("GP", [P, 2, 512]), "mx": ps("MX", [P, 2, 512]), "st": ps("ST", [P, 2, 512]),
              "ot": ps("OT", [P, 2, 512])}

        lines = nc.dram_tensor("lines", [6, H, LINE], F32, kind="Internal").ap()

        def signal(name, labels):
            return {"sem": sem(name), "at": {x: i + 1 for i, x in enumerate(labels)}, "n": len(labels)}

        def of(chain, kinds, engine=None):
            return [s for s in {"A": CHAIN_A, "B": CHAIN_B}[chain]
                    if s[0] in kinds and (engine is None or GENERAL[s[0]] == engine)]

        LN = {"A": ["E1", "E2", "L0"], "B": ["D1", "D2", "D3"]}
        ln_tiles = {l: 1 if l[0] == "E" else TQ for c in "AB" for l in LN[c]}
        ln_labels = {c: [(l, t) for l in LN[c] for t in range(ln_tiles[l])] for c in "AB"}
        pre_labels = {"A": ["enc_bo", "xa_bo", "enc_ff2"], "B": ["sa_bo", "ca_bo", "dec_ff2"]}
        biased = {c: [s for s in of(c, ["st"]) if s[1] != XA] for c in "AB"}
        full = {c: signal("full" + c, of(c, list(GENERAL) + ["mx", "st", "pv"])) for c in "AB"}
        act_done = {c: signal("act_done" + c, of(c, GENERAL, "act")) for c in "AB"}
        dve_done = {c: signal("dve_done" + c, of(c, GENERAL, "dve")) for c in "AB"}
        mx_done = {c: signal("mx_done" + c, of(c, ["mx"])) for c in "AB"}
        st_biased = {c: signal("st_biased" + c, biased[c]) for c in "AB"}
        p_ready = {c: signal("p_ready" + c, of(c, ["st"])) for c in "AB"}
        oc_ready = {c: signal("oc_ready" + c, of(c, ["pv"])) for c in "AB"}
        den_ready = {c: signal("den_ready" + c, of(c, ["tq"])) for c in "AB"}
        qr_ready = {c: signal("qr_ready" + c, of(c, ["q"])) for c in "AB"}
        km_ready, kr_ready = ({c: signal(n + c, [(s, j) for s in of(c, ["k"]) for j in range(KC)]) for c in "AB"}
                              for n in ("km_ready", "kr_ready"))
        stats = {c: signal("stats" + c, ln_labels[c]) for c in "AB"}
        aggr = {c: signal("aggr" + c, ln_labels[c]) for c in "AB"}
        eps_added = {c: signal("eps_added" + c, LN[c]) for c in "AB"}
        rstd_ready = {c: signal("rstd_ready" + c, LN[c]) for c in "AB"}
        xn_ready = {c: signal("xn_ready" + c, ln_labels[c]) for c in "AB"}
        pre_added = {c: signal("pre_added" + c, pre_labels[c]) for c in "AB"}
        affine = signal("affine", ["gamma", "beta"])
        chain_of_signal = {id(v[c]): c for v in (full, act_done, dve_done, mx_done, st_biased, p_ready, oc_ready,
                                                 den_ready, qr_ready, km_ready, kr_ready, stats, aggr, eps_added, rstd_ready,
                                                 xn_ready, pre_added) for c in "AB"}
        chain_of_signal[id(affine)] = "B"
        c_loaded, x_loaded, stored = ({"sem": sem(n), "at": {n: 16}, "n": 16} for n in ("c_loaded", "x_loaded", "stored"))
        chain_of_signal |= {id(c_loaded): "A", id(x_loaded): "A", id(stored): "B"}
        credited = {
            "vector": [dve_done["B"], mx_done["B"], st_biased["B"], den_ready["B"], stats["B"], aggr["B"], xn_ready["B"],
                       qr_ready["B"], km_ready["B"], affine],
            "scalar": [act_done["B"], p_ready["B"], oc_ready["B"], kr_ready["B"]],
            "tensor": [full["B"]],
            "gpsimd": [eps_added["B"], rstd_ready["B"], pre_added["B"]],
            "sync": [stored],
        }
        w_loaded, built, lines_out, toep = sem("w_loaded"), sem("built"), sem("lines_out"), sem("toep")
        bv_spread, bo_full, bo_added = sem("bv_spread"), sem("bo_full"), sem("bo_added")
        made, ident_made, flip_made = sem("made"), sem("ident_made"), sem("flip_made")
        flip_full, flip_out, zeroed = sem("flip_full"), sem("flip_out"), sem("zeroed")
        settled = {nc.vector: sem("dve_settled"), nc.gpsimd: sem("pool_settled"), nc.sync: sem("sp_settled")}

        block = stack.enter_context(nc.Block())

        def wait(eng, sig, label, it, now=True):
            c = chain_of_signal[id(sig)]
            if isinstance(it, int):
                if it == -1 and (c == "B" or not now):
                    return
                assert not (it == NB - 1 and c == "A" and now)
            eng.wait_ge(sig["sem"], it * sig["n"] + (sig["n"] if now else 0) + sig["at"][label])

        def wait_place(eng, step, it, phase):
            r = RING_OF[step]
            was, same = before(step, r, NBANK[r], phase)
            if was is None:
                return
            c = CHAIN[was]
            if r == "gp":
                sig = {"act": act_done, "dve": dve_done, "dve keys": km_ready}[GENERAL[was[0]]][c]
                was = (was, KC - 1) if was[0] == "k" else was
            elif r == "mx":
                sig = mx_done[c]
            elif r == "ot":
                sig = oc_ready[c]
            else:
                sig = (p_ready if was[1] == XA else st_biased)[c]
            wait(eng, sig, was, it, same)

        def bank(step):
            r = RING_OF[step]
            return PS[r][:, RINGS[r].index(step) % NBANK[r], :]

        def passes(eng, body):
            body(-1, "A")
            with eng.Fori(0, NB - 1) as it:
                body(it, "AB")
            body(NB - 1, "B")

        def steps(phase):
            return [s for s in ORDER if CHAIN[s] in phase]

        def settle(eng):
            eng.sem_inc(settled[eng], 1)

        def col(name, c):
            return col_sb[:, COL[name] + c:COL[name] + c + 1]

        REL = [ENC, SA, CA]
        prw = PR[:].rearrange("p s n -> p (s n)")
        rel_sb = prw[0:H, 0:3 * 512].rearrange("h (r d e) -> h r d e", r=3, d=2)
        stage_big = w_stage = KM["B"][:].rearrange("p c v n -> p (c v n)")
        homes = [b[0:H].rearrange("h c n -> h (c n)")[:, 0:LINE] for b in (XN["A"], XN["B"], OC["A"], OC["B"], XT, YT)]
        tables = []
        for a in REL:
            w = LK if a == ENC else LQ
            tables += [(tk[a], w, 0), (tq[a], w, P if a == ENC else 0)]
        flip = Y[:, 0, 0:P]
        N_ZEROED = 11
        HB = 8

        def block_heads(w):
            return 4 if w == LK else 2

        N_FLIP = sum(H // block_heads(w) for _, w, _ in tables)

        def line(i):
            return homes[i]

        def bv_cols(a, c):
            return XT[:].rearrange("p c n -> p (c n)")[:, P * c:P * (c + 1)] if a % 2 == 0 else (
                YT[:].rearrange("p c n -> p (c n)")[:, P * c:P * (c + 1)])

        @block.sync
        def _(sp):
            sp.dma_start(w_sb[:].rearrange("p m c n -> p m (c n)"), wm).then_inc(w_loaded, 16)
            sp.dma_start(ff1_sb[:].rearrange("p m c n -> p m (c n)"), wff1).then_inc(w_loaded, 16)
            sp.dma_start(ff2_sb[:].rearrange("p m c n -> p m (c n)"), wff2).then_inc(w_loaded, 16)
            sp.dma_start(col_sb[:], cols).then_inc(w_loaded, 16)
            sp.dma_start(row_sb[:].rearrange("p r d -> p (r d)"),
                         bass.AP(rows.tensor, 0, [[0, P], [1, len(ROWS) * D]])).then_inc(w_loaded, 16)
            for r in range(3):
                sp.dma_start(rel_sb[:, r, 0, :], rel_up[r]).then_inc(toep, 16)
                sp.dma_start(rel_sb[:, r, 1, :], rel_down[r]).then_inc(toep, 16)
            sp.wait_ge(built, 6)
            for i in range(6):
                sp.dma_start(lines[i], line(i)).then_inc(lines_out, 16)
            sp.wait_ge(lines_out, 96)
            done = 0
            for j, (tab, w, off) in enumerate(tables):
                for h0 in range(0, H, HB):
                    if done:
                        sp.wait_ge(flip_out, done)
                    sp.dma_start(stage_big[:, 0:HB * w].rearrange("p (h w) -> p h w", h=HB),
                                 bass.AP(lines.tensor, j * H * LINE + h0 * LINE + off,
                                         [[1, P], [LINE, HB], [1, w]])).then_inc(toep, 16)
                    done += HB // block_heads(w)
            for s in credited["sync"]:
                sp.sem_inc(s["sem"], s["n"])

            def body(it, phase):
                if "A" in phase:
                    wait(sp, full["A"], ("mem",), it, False)
                    settle(sp)
                    nb = it + 1
                    sp.dma_start(C[0:LK, :, :], ctxt[bass.ds(nb, 1)].rearrange("b k d -> k b d")).then_inc(c_loaded["sem"], 16)
                    wait(sp, xn_ready["A"], ("L0", TQ - 1), it, False)
                    settle(sp)
                    sp.dma_start(X[:], x[bass.ds(nb, 1)].rearrange("b (t p) d -> p (b t) d", p=P)).then_inc(x_loaded["sem"], 16)
                if "B" in phase:
                    wait(sp, dve_done["B"], ("f2", "B"), it)
                    settle(sp)
                    sp.dma_start(out[bass.ds(it, 1)].rearrange("b (t p) d -> p (b t) d", p=P), Y[:]).then_inc(stored["sem"], 16)

            passes(sp, body)
            wait(sp, stored, "stored", NB - 1)

        @block.tensor
        def _(pe):
            mm, tr = nc.tensor.matmul, nc.tensor.transpose
            pe.wait_ge(w_loaded, 80)
            pe.wait_ge(ident_made, 4)
            pe.wait_ge(made, 2)
            pe.wait_ge(zeroed, N_ZEROED)
            pe.wait_ge(flip_made, 2)
            n_block = n_load = 0
            for tab, w, _ in tables:
                nh = block_heads(w)
                for h0 in range(0, H, HB):
                    n_load += 1
                    pe.wait_ge(toep, 16 * (6 + n_load))
                    for q in range(HB // nh):
                        n_block += 1
                        if n_block > 2:
                            pe.wait_ge(flip_out, n_block - 2)
                        mm(PS["gp"][:, n_block % 2, 0:nh * w], flip, stage_big[:, nh * w * q:nh * w * (q + 1)],
                           start=True, stop=True).then_inc(flip_full, 1)
            pe.wait_ge(flip_out, N_FLIP)
            for a in range(4):
                pe.wait_ge(bv_spread, a + 1)
                if a >= 2:
                    pe.wait_ge(bo_added, a - 1)
                for c in range(KC):
                    i = mm(PS["gp"][:, a % 2, 0:D], bv_cols(a, c), w_sb[:, 4 * a + 3, c, :], start=c == 0, stop=c == KC - 1)
                i.then_inc(bo_full, 1)
            pe.wait_ge(bo_added, 4)
            for s in credited["tensor"]:
                pe.sem_inc(s["sem"], s["n"])

            def transposes(b_, src, nt, n_tiles):
                for c in range(KC):
                    for t in range(n_tiles):
                        at = nt * (n_tiles * c + t)
                        i = tr(b_[:, at:at + nt], src[0:nt, t, P * c:P * (c + 1)], ident[0:nt, 0:nt])
                return i

            def project(b_, w, src, n):
                for c in range(KC):
                    for k in range(KC):
                        i = mm(b_[:, n * c:n * (c + 1)], w[:, k, P * c:P * (c + 1)], src[:, k, 0:n],
                               start=k == 0, stop=k == KC - 1)
                return i

            def project_tokens(b_, w, src, nt, n_tiles, n_k=KC):
                for t in range(n_tiles):
                    for k in range(n_k):
                        i = mm(b_[0:nt, D * t:D * (t + 1)], src[:, k, nt * t:nt * (t + 1)], w[:, k, :],
                               start=k == 0, stop=k == n_k - 1)
                return i

            def body(it, phase):
                for s in steps(phase):
                    kind, ch = s[0], CHAIN[s]
                    if s not in RING_OF:
                        continue
                    a = s[1] if len(s) > 1 else None
                    b_ = bank(s)
                    if kind in ("q", "k", "v", "mt", "o", "mx", "st", "pv", "tq", "tc"):
                        nt = LK if a == ENC else P
                        nk = key_tile(a)
                        src_q = {ENC: ET, XA: XT, SA: YT, CA: YT}[a]
                        src_k = {ENC: ET, XA: CT, SA: YT, CA: MEMT}[a]
                    if kind == "ct":
                        wait(pe, c_loaded, "c_loaded", it)
                    elif kind == "xt":
                        wait(pe, x_loaded, "x_loaded", it)
                    elif kind == "et":
                        wait(pe, xn_ready["A"], ("E1" if a == ENC else "E2", 0), it)
                    elif kind == "yt":
                        wait(pe, xn_ready["B"], ({SA: "D1", CA: "D2", "ff": "D3"}[a], TQ - 1), it)
                    elif kind == "mem":
                        wait(pe, dve_done["A"], ("f2", "A"), it)
                    elif kind == "q":
                        wait(pe, act_done[ch], {ENC: ("et", ENC), XA: ("xt",), SA: ("yt", SA), CA: ("yt", CA)}[a], it)
                    elif kind == "k":
                        if a == CA:
                            wait(pe, act_done["A"], ("mem",), it, False)
                        else:
                            wait(pe, act_done[ch], {ENC: ("et", ENC), XA: ("ct",), SA: ("yt", SA)}[a], it)
                    elif kind == "mx" and s[2] == 0:
                        wait(pe, qr_ready[ch], ("q", a), it)
                        wait(pe, kr_ready[ch], (("k", a), KC - 1), it)
                    elif kind == "mt":
                        wait(pe, mx_done[ch], ("mx", a, len(max_tiles(a)) - 1), it)
                    elif kind == "st" and s[2] == 0:
                        wait(pe, act_done[ch], ("mt", a), it)
                    elif kind == "pv":
                        wait(pe, p_ready[ch], ("st", a, len(units(a)) * (s[2] + 1) // 4 - 1), it)
                        if s[2] == 0:
                            wait(pe, dve_done[ch], ("v", a), it)
                    elif kind == "tq" and s[2] == 0:
                        wait(pe, oc_ready[ch], ("pv", a, 3), it)
                    elif kind == "tc":
                        wait(pe, dve_done[ch], ("tq", a, query_tiles(a) - 1), it)
                    elif kind == "o":
                        wait(pe, act_done[ch], ("tc", a), it)
                    elif kind == "f1" and s[2] == 0:
                        wait(pe, act_done[ch], ("et" if ch == "A" else "yt", "ff"), it)
                    elif kind == "f2":
                        wait(pe, act_done[ch], ("f1", ch, 1 if ch == "A" else 3), it)
                    wait_place(pe, s, it, phase)
                    if kind == "ct" or kind == "mem":
                        i = transposes(b_, C, LK, 1)
                    elif kind == "xt":
                        i = transposes(b_, X, P, TQ)
                    elif kind == "et":
                        i = transposes(b_, XE, LK, 1)
                    elif kind == "yt":
                        i = transposes(b_, XN["B"], P, TQ)
                    elif kind == "q":
                        i = project(b_, w_sb[:, 4 * a], src_q, queries(a))
                    elif kind == "k":
                        i = project(b_, w_sb[:, 4 * a + 1], src_k, keys(a))
                    elif kind == "v":
                        i = project_tokens(b_, w_sb[:, 4 * a + 2], src_k, nk, keys(a) // nk)
                    elif kind == "mx":
                        t, g, v, nh, n_keys = max_tiles(a)[s[2]]
                        c, r = divmod(g, 2)
                        o = b_[0:nt, 0:nh * n_keys].rearrange("p (h k) -> p h k", h=nh)
                        if a != XA:
                            h0, j0 = 4 * g + v, 0 if a == ENC else P - P * t
                            mm(o, identb[0:nt, 0:nt], tq[a][0:nt, h0:h0 + nh, j0:j0 + n_keys], start=True, stop=False)
                        i = mm(o, QR[ch][:, c, r, P * t:P * t + nt], KR[ch][:, c, v:v + nh, 0:n_keys],
                               start=a == XA, stop=True)
                    elif kind == "mt":
                        for t in range(query_tiles(a)):
                            i = tr(b_[0:MR, P * t:P * t + nt], NM[ch][0:nt, t, :], ident[0:nt, 0:nt])
                    elif kind == "st":
                        g, v0, nh, kt, q0, nq = units(a)[s[2]]
                        c, r = divmod(g, 2)
                        for j in range(nh):
                            o = b_[0:nk, nq * j:nq * (j + 1)]
                            at = 64 * r + 4 * c + v0 + j
                            mm(o, identb[:, at:at + 1].broadcast_to([P, nk]), MT[ch][:, q0:q0 + nq], start=True, stop=False)
                            i = mm(o, KM[ch][:, c, v0 + j, P * kt:P * kt + nk], QT[ch][:, c, r, q0:q0 + nq],
                                   start=False, stop=True)
                    elif kind == "pv":
                        us = [(u, x) for u, x in enumerate(units(a)) if x[0] == s[2]]
                        for kt in range(keys(a) // nk):
                            for v in range(4):
                                u, (_, v0, nh, _, q0, nq) = next(
                                    (u, x) for u, x in us if x[3] == kt and x[1] <= v < x[1] + x[2])
                                i = mm(b_[32 * v:32 * v + HD + 1, q0:q0 + nq], V[ch][0:nk, kt, 4 * s[2] + v, :],
                                       PR[0:nk, unit_slot(a, u), nq * (v - v0):nq * (v - v0 + 1)],
                                       start=kt == 0, stop=kt == keys(a) // nk - 1, tile_position=(0, 32 * v))
                    elif kind == "tq":
                        for g in range(4):
                            i = tr(b_[0:nt, P * g:P * (g + 1)], OC[ch][:, g, P * s[2]:P * s[2] + nt], ident[:])
                    elif kind == "tc":
                        i = transposes(b_, CN[ch], nt, query_tiles(a))
                    elif kind == "o":
                        i = project_tokens(b_, w_sb[:, 4 * a + 3], src_q, nt, query_tiles(a))
                    elif kind == "f1":
                        e, n = (0, LK) if ch == "A" else (1, LQ)
                        per = FC // 2 if ch == "A" else FC // 4
                        src = ET if ch == "A" else YT
                        for m in range(per):
                            for k in range(KC):
                                at = P * (per * s[2] + m)
                                i = mm(b_[:, n * m:n * (m + 1)], ff1_sb[:, e, k, at:at + P], src[:, k, :],
                                       start=k == 0, stop=k == KC - 1)
                    elif kind == "f2":
                        e, nt, n_t = (0, LK, 1) if ch == "A" else (1, P, TQ)
                        i = project_tokens(b_, ff2_sb[:, e], HID[ch], nt, n_t, FC)
                    i.then_inc(full[ch]["sem"], 1)

            passes(pe, body)

        @block.scalar
        def _(act):
            copy = nc.scalar.copy
            n_block = 0
            for tab, w, _ in tables:
                nh = block_heads(w)
                for q in range(H // nh):
                    n_block += 1
                    act.wait_ge(flip_full, n_block)
                    copy(tab[:, nh * q:nh * (q + 1), :],
                         PS["gp"][:, n_block % 2, 0:nh * w].rearrange("p (h w) -> p h w", h=nh)).then_inc(flip_out, 1)
            act.wait_ge(w_loaded, 80)
            for s in credited["scalar"]:
                act.sem_inc(s["sem"], s["n"])

            def affine_features(b_, dst, scale, bias):
                n = dst.shape[2]
                for c in range(KC):
                    i = nc.scalar.activation(dst[:, c, :], b_[:, n * c:n * (c + 1)], ACT.Identity, bias=col(bias, c),
                                             scale=col(scale, c))
                return i

            def body(it, phase):
                for s in steps(phase):
                    kind, ch = s[0], CHAIN[s]
                    a = s[1] if len(s) > 1 else None
                    if kind == "st":
                        g, v0, nh, kt, q0, nq = units(a)[s[2]]
                        dst = PR[0:key_tile(a), unit_slot(a, s[2]), 0:nh * nq]
                        src = dst
                        if a == XA:
                            wait(act, full[ch], s, it)
                            src = bank(s)[0:LK, 0:nh * nq]
                        else:
                            wait(act, st_biased[ch], s, it)
                        nc.scalar.activation(dst, src, ACT.Exp).then_inc(p_ready[ch]["sem"], 1)
                        continue
                    if kind == "pv":
                        wait(act, full[ch], s, it)
                        nq = queries(a)
                        copy(OC[ch][:, s[2], 0:nq], bank(s)[:, 0:nq]).then_inc(oc_ready[ch]["sem"], 1)
                        continue
                    if GENERAL.get(kind) != "act" and kind != "k":
                        continue
                    if kind == "k":
                        w = keys(a)
                        for c in range(KC):
                            wait(act, km_ready[ch], (s, c), it)
                            copy(KR[ch][:, c, :, 0:w], KM[ch][:, c, :, 0:w]).then_inc(kr_ready[ch]["sem"], 1)
                        continue
                    b_ = bank(s)
                    wait(act, full[ch], s, it)
                    if kind in ("ct", "xt", "mem", "tc"):
                        dst = {"ct": CT, "xt": XT, "mem": MEMT}.get(kind) or (ET if a == ENC else XT if a == XA else YT)
                        n = dst.shape[2]
                        if kind == "mem":
                            wait(act, full["B"], ("v", CA), it)
                        i = copy(dst[:].rearrange("p c n -> p (c n)"), b_[:, 0:KC * n])
                    elif kind == "et":
                        n = "1" if a == ENC else "2"
                        i = affine_features(b_, ET[:], f"enc_n{n}_s", f"enc_n{n}_b")
                    elif kind == "yt":
                        n = {SA: "1", CA: "2", "ff": "3"}[a]
                        i = affine_features(b_, YT[:], f"dec_n{n}_s", f"dec_n{n}_b")
                    elif kind == "q":
                        w = queries(a)
                        for c in range(KC):
                            for r in range(2):
                                half = slice(64 * r, 64 * r + 64)
                                i = nc.scalar.activation(QT[ch][half, c, r, 0:w], b_[half, w * c:w * (c + 1)], ACT.Identity,
                                                         bias=col(PRE[a] + "_bq", c)[half], scale=1.0)
                    elif kind == "mt":
                        nq = queries(a)
                        i = copy(MT[ch][0:MR, 0:nq], b_[0:MR, 0:nq])
                    elif kind == "f1":
                        n, per = (LK, FC // 2) if ch == "A" else (LQ, FC // 4)
                        for m in range(per):
                            mi = per * s[2] + m
                            i = nc.scalar.activation(HID[ch][:, mi, :], b_[:, n * m:n * (m + 1)], ACT.Relu,
                                                     bias=col("enc_ff1" if ch == "A" else "dec_ff1", mi), scale=1.0)
                    i.then_inc(act_done[ch]["sem"], 1)

            passes(act, body)

        @block.vector
        def _(dve):
            tt, ts, cp = nc.vector.tensor_tensor, nc.vector.tensor_scalar, nc.vector.tensor_copy
            for c in "AB":
                nc.vector.memset(NM[c][:], 0.0).then_inc(zeroed, 1)
                nc.vector.memset(V[c][:], 1.0).then_inc(zeroed, 1)
                nc.vector.memset(MT[c][:], 0.0).then_inc(zeroed, 1)
                nc.vector.memset(QT[c][:], 0.0).then_inc(zeroed, 1)
                nc.vector.memset(QR[c][:], 0.0).then_inc(zeroed, 1)
            nc.vector.memset(PS["ot"][:], 0.0).then_inc(zeroed, 1)
            dve.wait_ge(toep, 96)
            for r in range(3):
                up, down = rel_sb[:, r, 0, :], rel_sb[:, r, 1, :]
                lk_, lq_ = line(2 * r), line(2 * r + 1)
                far = up[:, P - 1:P]
                if REL[r] == SA:
                    cp(lk_[:, P - 1:P], down[:, P - 1:P])
                    nc.vector.memset(lk_[:, 0:P - 1], MASKED)
                else:
                    cp(lk_[:, 0:P], down[:, 0:P])
                cp(lk_[:, P:2 * P - 1], up[:, 1:P])
                cp(lk_[:, 2 * P - 1:LINE], far.broadcast_to([H, LINE - 2 * P + 1])).then_inc(built, 1)
                cp(lq_[:, 0:P], far.broadcast_to([H, P]))
                cp(lq_[:, P:2 * P - 1], down[:, P:2 * P - 1])
                if REL[r] == SA:
                    nc.vector.memset(lq_[:, 2 * P:LINE], MASKED)
                    cp(lq_[:, 2 * P - 1:2 * P], up[:, P:P + 1]).then_inc(built, 1)
                else:
                    nc.vector.memset(lq_[:, LINE - 1:LINE], 0.0)
                    cp(lq_[:, 2 * P - 1:LINE - 1], up[:, P:2 * P]).then_inc(built, 1)
            dve.wait_ge(ident_made, 3)
            cp(identb[:], ident[:]).then_inc(ident_made, 1)
            dve.wait_ge(ident_made, 4)
            nc.vector.tensor_reduce(head_mask[:], ident[:].rearrange("p (r v d) -> p v r d", r=2, v=4), AX.XY,
                                    ALU.add).then_inc(made, 1)
            dve.wait_ge(made, 1)
            ts(head_mask[:], head_mask[:], SCALE, None, ALU.mult).then_inc(made, 1)
            dve.wait_ge(made, 2)
            dve.wait_ge(w_loaded, 80)
            dve.wait_ge(flip_out, N_FLIP)
            for a in range(4):
                if a >= 2:
                    dve.wait_ge(bo_full, a - 1)
                for c in range(KC):
                    i = cp(bv_cols(a, c), col(PRE[a] + "_bv", c).broadcast_to([P, P]))
                i.then_inc(bv_spread, 1)
            for a in range(4):
                dve.wait_ge(bo_full, a + 1)
                bo = row_sb[:, ROW[PRE[a] + "_bo"], :]
                tt(bo, PS["gp"][:, a % 2, 0:D], bo, ALU.add).then_inc(bo_added, 1)
            dve.wait_ge(zeroed, N_ZEROED)
            for s in credited["vector"]:
                dve.sem_inc(s["sem"], s["n"])

            def normalise(l, ch, it):
                src, dst, np_ = {"E": (C, XE, LK), "L": (X, XN["A"], P), "D": (Y, XN["B"], P)}[l[0]]
                source = {"E1": (c_loaded, "c_loaded"), "E2": (dve_done["A"], ("o", ENC)), "L0": (dve_done["A"], ("o", XA)),
                          "D1": (affine, "beta"), "D2": (dve_done["B"], ("o", SA)), "D3": (dve_done["B"], ("o", CA))}[l]
                wait(dve, *source, it)
                for t in range(ln_tiles[l]):
                    nc.vector.bn_stats(st6[ch][0:np_, t, :], src[0:np_, t, :]).then_inc(stats[ch]["sem"], 1)
                wait(dve, stats[ch], (l, ln_tiles[l] - 1), it)
                settle(dve)
                for t in range(ln_tiles[l]):
                    nc.vector.bn_aggr(mv[ch][0:np_, t, :], st6[ch][0:np_, t, :]).then_inc(aggr[ch]["sem"], 1)
                wait(dve, rstd_ready[ch], l, it)
                for t in range(ln_tiles[l]):
                    ts(dst[0:np_, t, :], src[0:np_, t, :], mv[ch][0:np_, t, 0:1], rstd[ch][0:np_, t:t + 1],
                       ALU.subtract, ALU.mult).then_inc(xn_ready[ch]["sem"], 1)

            def body(it, phase):
                for s in steps(phase):
                    kind, ch = s[0], CHAIN[s]
                    a = s[1] if len(s) > 1 else None
                    if kind == "affine":
                        gam = row_sb[:, ROW["gamma"]:ROW["gamma"] + 1, :].broadcast_to([P, TQ, D])
                        bet = row_sb[:, ROW["beta"]:ROW["beta"] + 1, :].broadcast_to([P, TQ, D])
                        wait(dve, xn_ready["A"], ("L0", TQ - 1), it, False)
                        wait(dve, stored, "stored", it, False)
                        tt(Y[:], XN["A"][:], gam, ALU.mult).then_inc(affine["sem"], 1)
                        wait(dve, affine, "gamma", it)
                        tt(Y[:], Y[:], bet, ALU.add).then_inc(affine["sem"], 1)
                    elif kind == "ln":
                        normalise(a, ch, it)
                    elif kind == "mx":
                        t, g, v, nh, n_keys = max_tiles(a)[s[2]]
                        c, r = divmod(g, 2)
                        nt, at = LK if a == ENC else P, 64 * r + 4 * c + v
                        wait(dve, full[ch], s, it)
                        nc.vector.tensor_reduce(NM[ch][0:nt, t, at:at + nh],
                                                bank(s)[0:nt, 0:nh * n_keys].rearrange("p (h k) -> p h k", h=nh),
                                                AX.X, ALU.max, negate=True).then_inc(mx_done[ch]["sem"], 1)
                    elif kind == "st" and a != XA:
                        g, v0, nh, kt, q0, nq = units(a)[s[2]]
                        nk, h0 = key_tile(a), 4 * g + v0
                        wait(dve, full[ch], s, it)
                        tt(PR[0:nk, unit_slot(a, s[2]), 0:nh * nq].rearrange("p (h q) -> p h q", h=nh),
                           bank(s)[0:nk, 0:nh * nq].rearrange("p (h q) -> p h q", h=nh),
                           tk[a][0:nk, h0:h0 + nh, 0:nq], ALU.add).then_inc(st_biased[ch]["sem"], 1)
                    elif kind == "q":
                        w = queries(a)
                        wait(dve, act_done[ch], s, it)
                        cp(QR[ch][:, :, :, 0:w], QT[ch][:, :, :, 0:w]).then_inc(qr_ready[ch]["sem"], 1)
                    elif GENERAL.get(kind, "act") != "act":
                        b_ = bank(s)
                        wait(dve, full[ch], s, it)
                        if kind == "k":
                            w = keys(a)
                            for c in range(KC):
                                for v in range(4):
                                    i = ts(KM[ch][:, c, v, 0:w], b_[:, w * c:w * (c + 1)], col(PRE[a] + "_bk", c),
                                           head_mask[:, v:v + 1], ALU.add, ALU.mult)
                                i.then_inc(km_ready[ch]["sem"], 1)
                            continue
                        elif kind == "v":
                            nk = key_tile(a)
                            n = keys(a) // nk
                            i = cp(V[ch][0:nk, 0:n, :, 0:HD],
                                   b_[0:nk, 0:D * n].rearrange("p (t h d) -> p t h d", t=n, h=H))
                        elif kind == "tq":
                            nt = LK if a == ENC else P
                            tqs = of(ch, ["tq"])
                            n = tqs.index(s)
                            rd = rden[ch][0:nt, n % 2, :].rearrange("p (h o) -> p h o", o=1)
                            o = b_[0:nt, :].rearrange("p (h d) -> p h d", d=32)
                            if n >= 2:
                                wait(dve, dve_done[ch], tqs[n - 2], it)
                            else:
                                prev = [x for i_, x in enumerate(tqs) if i_ % 2 == n % 2][-1]
                                wait(dve, dve_done[ch], prev, it, False)
                            if ch == "A" and n == 0:
                                wait(dve, affine, "gamma", it)
                            nc.vector.reciprocal(rd, o[:, :, HD:HD + 1]).then_inc(den_ready[ch]["sem"], 1)
                            wait(dve, den_ready[ch], s, it)
                            i = tt(CN[ch][0:nt, s[2], :].rearrange("p (h d) -> p h d", h=H), o[:, :, 0:HD],
                                   rd.broadcast_to([nt, H, HD]), ALU.mult)
                        elif kind in ("o", "f2"):
                            name = PRE[a] + "_bo" if kind == "o" else ("enc_ff2" if ch == "A" else "dec_ff2")
                            wait(dve, pre_added[ch], name, it)
                            dst = C[0:LK, :, :] if a in (ENC, "A") else X[:] if a == XA else Y[:]
                            np_, n_t, _ = dst.shape
                            i = tt(dst, b_[0:np_, 0:n_t * D].rearrange("p (t d) -> p t d", t=n_t), dst, ALU.add)
                        i.then_inc(dve_done[ch]["sem"], 1)

            passes(dve, body)

        @block.gpsimd
        def _(pool):
            nc.gpsimd.memset(ident[:], 0.0).then_inc(ident_made, 1)
            pool.wait_ge(ident_made, 1)
            nc.gpsimd.affine_select(out=ident[:], in_=ident[:], compare_op=ALU.not_equal, fill=1.0, base=0,
                                    pattern=[[-1, P]], channel_multiplier=1).then_inc(ident_made, 1)
            nc.gpsimd.memset(exponent[:], -0.5).then_inc(ident_made, 1)
            nc.gpsimd.memset(flip, 0.0).then_inc(flip_made, 1)
            pool.wait_ge(flip_made, 1)
            nc.gpsimd.affine_select(out=flip, in_=flip, compare_op=ALU.not_equal, fill=1.0, base=1 - P,
                                    pattern=[[1, P]], channel_multiplier=1).then_inc(flip_made, 1)
            pool.wait_ge(ident_made, 3)
            pool.wait_ge(w_loaded, 80)
            for s in credited["gpsimd"]:
                pool.sem_inc(s["sem"], s["n"])

            def inverse_deviation(l, ch, it):
                n_t, np_ = ln_tiles[l], LK if l[0] == "E" else P
                eps = EPS_L0 if l == "L0" else EPS_L1
                wait(pool, aggr[ch], (l, n_t - 1), it)
                settle(pool)
                nc.gpsimd.tensor_scalar(ve[ch][0:np_, 0:n_t], mv[ch][0:np_, 0:n_t, 1], eps, 1.0, ALU.add,
                                        ALU.mult).then_inc(eps_added[ch]["sem"], 1)
                wait(pool, eps_added[ch], l, it)
                nc.gpsimd.tensor_tensor(rstd[ch][0:np_, 0:n_t], ve[ch][0:np_, 0:n_t], exponent[0:np_, 0:n_t],
                                        ALU.pow).then_inc(rstd_ready[ch]["sem"], 1)

            def add_row(name, dst, ch):
                np_, n_t, _ = dst.shape
                r = row_sb[0:np_, ROW[name]:ROW[name] + 1, :].broadcast_to([np_, n_t, D])
                nc.gpsimd.tensor_tensor(dst, dst, r, ALU.add).then_inc(pre_added[ch]["sem"], 1)

            def body(it, phase):
                for s in steps(phase):
                    kind, ch = s[0], CHAIN[s]
                    a = s[1] if len(s) > 1 else None
                    if kind == "ln":
                        inverse_deviation(a, ch, it)
                    elif kind == "q":
                        if a == ENC:
                            wait(pool, full["A"], ("ct",), it)
                            wait(pool, xn_ready["A"], ("E1", 0), it)
                            add_row("enc_bo", C[0:LK, :, :], ch)
                            wait(pool, full["A"], ("xt",), it)
                            add_row("xa_bo", X[:], ch)
                        elif a == XA:
                            wait(pool, xn_ready["A"], ("E2", 0), it)
                            add_row("enc_ff2", C[0:LK, :, :], ch)
                        else:
                            wait(pool, xn_ready["B"], ("D1" if a == SA else "D2", TQ - 1), it)
                            add_row(PRE[a] + "_bo", Y[:], ch)
                    elif s == ("yt", "ff"):
                        wait(pool, xn_ready["B"], ("D3", TQ - 1), it)
                        add_row("dec_ff2", Y[:], ch)

            passes(pool, body)


_ATT = ["enc", "xa", "sa", "ca"]


def kernel(**inputs):
    import numpy as _np
    import concourse.bacc as _bacc
    from concourse import mybir as _mybir
    from concourse.bass_utils import run_bass_kernel_spmd as _run

    i = {k: _np.asarray(v) for k, v in inputs.items()}
    l0 = lambda k: i["L0_xattn_" + k]
    l1 = lambda k: i["L1_xattn_" + k]
    in_w = [l1("enc_in_w"), None, l1("dec_sa_in_w"), l1("dec_ca_in_w")]
    out_w = [l1("enc_out_w"), None, l1("dec_sa_out_w"), l1("dec_ca_out_w")]
    in_b = [l1("enc_in_b"), _np.concatenate([l0("bq"), l0("bk"), l0("bv")]), l1("dec_sa_in_b"), l1("dec_ca_in_b")]
    out_b = [l1("enc_out_b"), l0("bo"), l1("dec_sa_out_b"), l1("dec_ca_out_b")]
    mats = []
    for a in range(4):
        if in_w[a] is None:
            mats += [l0("Wq"), l0("Wk"), l0("Wv"), l0("Wo")]
        else:
            mats += [in_w[a][D * j:D * (j + 1)].T for j in range(3)] + [out_w[a].T]

    def chunks(m):
        return m.reshape(-1, P, m.shape[1]).transpose(1, 0, 2).reshape(P, -1)

    wm = _np.stack([chunks(m) for m in mats], 1)
    wff1 = _np.stack([chunks(l1("enc_ff1_w").T), chunks(l1("dec_ff1_w").T)], 1)
    wff2 = _np.stack([chunks(l1("enc_ff2_w").T), chunks(l1("dec_ff2_w").T)], 1)
    vecs = {}
    for a, p in enumerate(_ATT):
        vecs[p + "_bq"], vecs[p + "_bk"], vecs[p + "_bv"] = (in_b[a][D * j:D * (j + 1)] for j in range(3))
        vecs[p + "_bo"] = out_b[a]
    for k in ("enc_n1", "enc_n2", "dec_n1", "dec_n2", "dec_n3"):
        vecs[k + "_s"], vecs[k + "_b"] = l1(k + "_s"), l1(k + "_b")
    vecs["gamma"], vecs["beta"] = l0("ln_gamma"), l0("ln_beta")
    vecs["enc_ff2"], vecs["dec_ff2"] = l1("enc_ff2_b"), l1("dec_ff2_b")
    cols = _np.concatenate([vecs[k].reshape(-1, P).T for k in COLS]
                           + [l1("enc_ff1_b").reshape(-1, P).T, l1("dec_ff1_b").reshape(-1, P).T], 1)
    rows = _np.stack([vecs[k] for k in ROWS])
    rels = [l1("enc_rel"), l1("dec_rel_self"), l1("dec_rel_cross")]
    arrays = {"x": i["x"], "ctxt": i["ctx_1024"], "wm": wm, "wff1": wff1, "wff2": wff2, "cols": cols, "rows": rows,
              "rel_up": _np.stack([r.T for r in rels]), "rel_down": _np.stack([r[::-1].T for r in rels])}
    nc = _bacc.Bacc("TRN2", target_bir_lowering=False, num_devices=1)
    feed, args = {}, []
    for name, a in arrays.items():
        a = _np.ascontiguousarray(a)
        feed[f"in_{name}"] = a
        args.append(nc.dram_tensor(f"in_{name}", a.shape, _mybir.dt.from_np(a.dtype), kind="ExternalInput").ap())
    args.append(nc.dram_tensor("out_0", (NB, LQ, D), _mybir.dt.float32, kind="ExternalOutput").ap())
    build(nc, *args)
    r = _run(nc, [feed], core_ids=[0])
    return r.results[0]["out_0"]
```

```python
from contextlib import ExitStack

import concourse.bass as bass
from concourse import mybir

F32 = mybir.dt.float32
BF16 = mybir.dt.bfloat16
ALU = mybir.AluOpType
ACT = mybir.ActivationFunctionType
AX = mybir.AxisListType

NB, LQ, D = 64, 256, 256
LK = 120
H, HD = 16, 16
DFF = 1024
P = 128
KC = D // P
TQ = LQ // P
FC = DFF // P
SCALE = 1.0 / HD ** 0.5
MASKED = -1.0e30
EPS_L0, EPS_L1 = 1e-5, 1e-6
ENC, XA, SA, CA = range(4)

COLS = ["enc_bq", "enc_bk", "xa_bq", "xa_bk", "sa_bq", "sa_bk", "ca_bq", "ca_bk",
        "enc_bv", "xa_bv", "sa_bv", "ca_bv",
        "enc_n1_s", "enc_n1_b", "enc_n2_s", "enc_n2_b",
        "dec_n1_s", "dec_n1_b", "dec_n2_s", "dec_n2_b", "dec_n3_s", "dec_n3_b"]
COL = {name: KC * i for i, name in enumerate(COLS)}
COL["enc_ff1"] = KC * len(COLS)
COL["dec_ff1"] = COL["enc_ff1"] + FC
NCOL = COL["dec_ff1"] + FC
ROWS = ["enc_bo", "xa_bo", "sa_bo", "ca_bo", "enc_ff2", "dec_ff2", "gamma", "beta"]
ROW = {name: i for i, name in enumerate(ROWS)}
PRE = ["enc", "xa", "sa", "ca"]
LINE = 384


def queries(a):
    return LK if a == ENC else LQ


def key_tile(a):
    return P if a == SA else LK


def keys(a):
    return LQ if a == SA else LK


def query_tiles(a):
    return 1 if a == ENC else TQ


def units(a):
    if a == ENC:
        return [(g, 0, 4, 0, 0, LK) for g in range(4)]
    return [x for g in range(4) for x in [(g, 0, 2, 0, 0, LQ), (g, 2, 2, 0, 0, LQ)]
            + [(g, 0, 4, 1, P, LQ - P)] * (a == SA)]


def max_tiles(a):
    if a == ENC:
        return [(0, g, 0, 4, LK) for g in range(4)]
    if a != SA:
        return [(t, g, 0, 4, LK) for t in range(TQ) for g in range(4)]
    return ([(0, g, 0, 4, P) for g in range(4)]
            + [(1, 2 * c + r, v, 2, 2 * P) for c in range(2) for v in (0, 2) for r in range(2)])


SCHEDULE = """
    ln.E1 f1.B.0 ln.D1 f1.B.1 nx.D1 nx.E1 f1.B.2 f1.B.3 xt ct et.ENC yt.SA k.ENC f2.B.0 q.ENC q.SA f2.B.1 mx.ENC.0
    mx.ENC.1 k.SA v.SA mx.ENC.2 mx.ENC.3 v.ENC mx.SA.0 mt.ENC mx.SA.1 st.ENC.0 mx.SA.2 mx.SA.3 st.ENC.1 mx.SA.4
    pv.ENC.0 mx.SA.5 st.ENC.2 mx.SA.6 mx.SA.7 st.ENC.3 mx.SA.8 mx.SA.9 pv.ENC.1 pv.ENC.2 mx.SA.10 pv.ENC.3 mx.SA.11
    tq.ENC.0 mt.SA tc.ENC st.SA.0 st.SA.1 st.SA.2 st.SA.3 st.SA.4 pv.SA.0 o.ENC ln.E2 st.SA.5 nx.E2 st.SA.6 st.SA.7
    et.ff k.XA pv.SA.1 st.SA.8 st.SA.9 q.XA st.SA.10 pv.SA.2 st.SA.11 mx.XA.0 mx.XA.1 f1.A.0 pv.SA.3 mx.XA.2 mx.XA.3
    v.XA tq.SA.0 mx.XA.4 tq.SA.1 mx.XA.5 f1.A.1 mx.XA.6 mx.XA.7 tc.SA mt.XA o.SA ln.D2 st.XA.0 k.CA nx.D2 f2.A.0
    v.CA yt.CA st.XA.1 q.CA st.XA.2 pv.XA.0 st.XA.3 mx.CA.0 mx.CA.1 mx.CA.2 mx.CA.3 pv.XA.1 mx.CA.4 mx.CA.5 st.XA.4
    mx.CA.6 mx.CA.7 st.XA.5 mt.CA st.XA.6 st.CA.0 st.CA.1 st.CA.2 st.CA.3 pv.CA.0 st.CA.4 st.CA.5 pv.CA.1 st.CA.6
    st.CA.7 pv.XA.2 st.XA.7 pv.CA.2 pv.CA.3 pv.XA.3 tq.CA.0 tq.CA.1 tq.XA.0 tc.CA tq.XA.1 o.CA ln.D3 nx.D3 tc.XA
    o.XA ln.L0 yt.ff mem nx.L0 affine
"""
LAG = {"A": 0, "B": 1, "T": 2}


def parse(word):
    names = {"ENC": ENC, "XA": XA, "SA": SA, "CA": CA}
    kind, *rest = word.split(".")
    return (kind, *(names[x] if x in names else int(x) if x.isdigit() else x for x in rest))


def chain_of_step(s):
    if s[0] in ("f1", "f2"):
        return "A" if s[1] == "A" else "T"
    if s[0] in ("ct", "xt", "et", "mem", "affine") or s[1] in (ENC, XA, "E1", "E2", "L0"):
        return "A"
    return "B"


ORDER = [parse(word) for word in SCHEDULE.split()]
CHAIN = {s: chain_of_step(s) for s in ORDER}
GENERAL = {"ct": "act", "xt": "act", "et": "act", "yt": "act", "mem": "act", "q": "act", "k": "dve keys", "v": "act",
           "mt": "act", "tq": "dve", "tc": "act", "o": "dve", "f1": "act", "f2": "dve"}
NBANK = {"gp": 2, "mx": 2, "st": 2, "ot": 2}


def ring(kinds):
    return [s for s in ORDER if s[0] in kinds]


RINGS = {"gp": ring(GENERAL), "mx": ring(["mx"]), "st": ring(["st"]), "ot": ring(["pv"])}
RING_OF = {s: r for r, xs in RINGS.items() for s in xs}
MR = 64 + 8
SLOTS = {"A": 3, "B": 5}
UNITS = {c: [s for s in ORDER if s[0] == "st" and CHAIN[s] == c] for c in "AB"}
assert all(len(UNITS[c]) % SLOTS[c] == 0 for c in "AB")


def before(step, ring_name, size, phase):
    xs = RINGS[ring_name]
    at = xs.index(step)
    for i in range(at - 1, -1, -1):
        if i % size == at % size and CHAIN[xs[i]] in phase:
            return xs[i], True
    was = {"A": "", "AB": "A", "ABT": "ABT", "BT": "ABT", "T": "BT"}[phase]
    for i in range(len(xs) - 1, -1, -1):
        if i % size == at % size and CHAIN[xs[i]] in was:
            return xs[i], False
    return None, False


def unit_slot(a, u):
    c = CHAIN[("st", a, u)]
    return 3 * (c == "B") + UNITS[c].index(("st", a, u)) % SLOTS[c]


def value_step(a, u):
    return ("pv", a, 4 * u // len(units(a)))


for c in "AB":
    for was, s in zip(UNITS[c], UNITS[c][SLOTS[c]:]):
        assert ORDER.index(value_step(*was[1:])) < ORDER.index(s), (was, s)
for first, then in [(("k", CA), ("mem",)), (("v", CA), ("mem",)), (("f1", "B", 3), ("yt", SA)),
                    (("f2", "B", TQ - 1), ("k", SA)), (("q", SA), ("tq", ENC, 0))]:
    assert ORDER.index(first) < ORDER.index(then), (first, then)


def build(nc, x, ctxt, wm, wff1, wff2, cols, rows, rel_up, rel_down, out):
    with ExitStack() as stack:
        def sb(name, shape, dt=F32):
            return stack.enter_context(nc.sbuf_tensor(name, shape, dt))

        def ps(name, shape):
            return stack.enter_context(nc.psum_tensor(name, shape, F32))

        def sem(name):
            return stack.enter_context(nc.semaphore(name))

        w_sb = sb("w_sb", [P, 16, KC, D])
        ff1_sb = sb("ff1_sb", [P, 2, KC, DFF])
        ff2_sb = sb("ff2_sb", [P, 2, FC, D])
        col_sb = sb("col_sb", [P, NCOL])
        row_sb = sb("row_sb", [P, len(ROWS), D])
        ident = sb("ident", [P, P])
        identb = sb("identb", [P, P], BF16)
        head_mask = sb("head_mask", [P, 4])
        exponent = sb("exponent", [P, TQ])
        tk = {ENC: sb("tk_enc", [P, H, LK]), SA: sb("tk_sa", [P, H, LQ]), CA: sb("tk_ca", [P, H, LQ])}
        tq = {ENC: sb("tq_enc", [P, H, LK], BF16), SA: sb("tq_sa", [P, H, LQ], BF16), CA: sb("tq_ca", [P, H, LQ], BF16)}
        X = sb("X", [P, TQ, D])
        C = sb("C", [P, 1, D])
        CT = sb("CT", [P, KC, LK])
        ET = sb("ET", [P, KC, LK])
        XT = sb("XT", [P, KC, LQ])
        MEMT = sb("MEMT", [P, KC, LK])
        Y = sb("Y", [P, TQ, D])
        YT = sb("YT", [P, KC, LQ])
        XN = {c: sb("XN" + c, [P, TQ, D]) for c in "AB"}
        CN = XN
        QT = {c: sb("QT" + c, [P, KC, 2, LQ]) for c in "AB"}
        QR = {c: sb("QR" + c, [P, KC, 2, LQ], BF16) for c in "AB"}
        KM = {c: sb("KM" + c, [P, KC, 4, w]) for c, w in (("A", LK), ("B", LQ))}
        KR = {c: sb("KR" + c, [P, KC, 4, w], BF16) for c, w in (("A", LK), ("B", LQ))}
        V = {c: sb("V" + c, [P, n, H, HD + 1]) for c, n in (("A", 1), ("B", 2))}
        OC = {c: sb("OC" + c, [P, 4, LQ]) for c in "AB"}
        XE = OC["A"][:, 0:1, :]
        NM = {c: sb("NM" + c, [P, TQ, MR]) for c in "AB"}
        MT = {c: sb("MT" + c, [P, LQ], BF16) for c in "AB"}
        HID = {"A": OC["A"][:].rearrange("p g n -> p (g n)")[:, 0:FC * LK].rearrange("p (m n) -> p m n", m=FC),
               "B": KM["B"][:].rearrange("p c v n -> p (c v) n")}
        PR = sb("PR", [P, sum(SLOTS.values()), 512])
        st6 = {c: sb("st6" + c, [P, TQ, 6]) for c in "AB"}
        mv = {c: sb("mv" + c, [P, TQ, 2]) for c in "AB"}
        ve = {c: sb("ve" + c, [P, TQ]) for c in "AB"}
        rstd = {c: sb("rstd" + c, [P, TQ]) for c in "AB"}
        rden = {c: sb("rden" + c, [P, 2, H]) for c in "AB"}
        PS = {"gp": ps("GP", [P, 2, 512]), "mx": ps("MX", [P, 2, 512]), "st": ps("ST", [P, 2, 512]),
              "ot": ps("OT", [P, 2, 512])}

        lines = nc.dram_tensor("lines", [6, H, LINE], F32, kind="Internal").ap()

        def signal(name, labels):
            return {"sem": sem(name), "at": {x: i + 1 for i, x in enumerate(labels)}, "n": len(labels)}

        def of(chain, kinds, engine=None):
            return [s for s in ORDER if CHAIN[s] == chain
                    and s[0] in kinds and (engine is None or GENERAL[s[0]] == engine)]

        LN = {"A": ["E1", "E2", "L0"], "B": ["D1", "D2", "D3"]}
        ln_tiles = {l: 1 if l[0] == "E" else TQ for c in "AB" for l in LN[c]}
        ln_labels = {c: [(l, t) for l in LN[c] for t in range(ln_tiles[l])] for c in "AB"}
        pre_labels = {"A": ["enc_bo", "enc_ff2", "xa_bo"], "B": ["sa_bo", "ca_bo", "dec_ff2"]}
        biased = {c: [s for s in of(c, ["st"]) if s[1] != XA] for c in "AB"}
        full = {c: signal("full" + c, of(c, list(GENERAL) + ["mx", "st", "pv"])) for c in "ABT"}
        act_done = {c: signal("act_done" + c, of(c, GENERAL, "act")) for c in "ABT"}
        dve_done = {c: signal("dve_done" + c, of(c, GENERAL, "dve")) for c in "ABT"}
        mx_done = {c: signal("mx_done" + c, of(c, ["mx"])) for c in "AB"}
        st_biased = {c: signal("st_biased" + c, biased[c]) for c in "AB"}
        p_ready = {c: signal("p_ready" + c, of(c, ["st"])) for c in "AB"}
        oc_ready = {c: signal("oc_ready" + c, of(c, ["pv"])) for c in "AB"}
        den_ready = {c: signal("den_ready" + c, of(c, ["tq"])) for c in "AB"}
        qr_ready = {c: signal("qr_ready" + c, of(c, ["q"])) for c in "AB"}
        km_ready, kr_ready = ({c: signal(n + c, [(s, j) for s in of(c, ["k"]) for j in range(KC)]) for c in "AB"}
                              for n in ("km_ready", "kr_ready"))
        stats = {c: signal("stats" + c, ln_labels[c]) for c in "AB"}
        aggr = {c: signal("aggr" + c, ln_labels[c]) for c in "AB"}
        eps_added = {c: signal("eps_added" + c, LN[c]) for c in "AB"}
        rstd_ready = {c: signal("rstd_ready" + c, LN[c]) for c in "AB"}
        xn_ready = {c: signal("xn_ready" + c, ln_labels[c]) for c in "AB"}
        pre_added = {c: signal("pre_added" + c, pre_labels[c]) for c in "AB"}
        affine = signal("affine", ["gamma", "beta"])
        chain_of_signal = {id(v[c]): c for v in (full, act_done, dve_done, mx_done, st_biased, p_ready, oc_ready,
                                                 den_ready, qr_ready, km_ready, kr_ready, stats, aggr, eps_added,
                                                 rstd_ready, xn_ready, pre_added) for c in v}
        chain_of_signal[id(affine)] = "A"
        c_loaded, x_loaded, stored = ({"sem": sem(n), "at": {n: 16}, "n": 16} for n in ("c_loaded", "x_loaded", "stored"))
        chain_of_signal |= {id(c_loaded): "A", id(x_loaded): "A", id(stored): "T"}
        credited = {
            "vector": [dve_done, mx_done, st_biased, den_ready, stats, aggr, xn_ready, qr_ready, km_ready],
            "scalar": [act_done, p_ready, oc_ready, kr_ready],
            "tensor": [full],
            "gpsimd": [eps_added, rstd_ready, pre_added],
            "sync": [{"T": stored}],
        }
        w_loaded, built, lines_out, toep = sem("w_loaded"), sem("built"), sem("lines_out"), sem("toep")
        bv_spread, bo_full, bo_added = sem("bv_spread"), sem("bo_full"), sem("bo_added")
        staged = [sem("staged0"), sem("staged1")]
        head_mask_made, ident_made, flip_made = sem("head_mask_made"), sem("ident_made"), sem("flip_made")
        flip_full, flip_out, zeroed = sem("flip_full"), sem("flip_out"), sem("zeroed")
        settled = {nc.vector: sem("dve_settled"), nc.gpsimd: sem("pool_settled"), nc.sync: sem("sp_settled")}

        block = stack.enter_context(nc.Block())

        def wait(eng, sig, label, it, now=True):
            c = chain_of_signal[id(sig)]
            if isinstance(it, int):
                batch = it + now - LAG[c]
                if batch < 0:
                    return
                assert batch < NB, (label, it)
            eng.wait_ge(sig["sem"], it * sig["n"] + (sig["n"] if now else 0) + sig["at"][label])

        def credit(eng, name):
            for sigs in credited[name]:
                for c in sigs:
                    if c != "A":
                        eng.sem_inc(sigs[c]["sem"], LAG[c] * sigs[c]["n"])

        def wait_place(eng, step, it, phase):
            r = RING_OF[step]
            was, same = before(step, r, NBANK[r], phase)
            if was is None:
                return
            c = CHAIN[was]
            if r == "gp":
                sig = {"act": act_done, "dve": dve_done, "dve keys": km_ready}[GENERAL[was[0]]][c]
                was = (was, KC - 1) if was[0] == "k" else was
            elif r == "mx":
                sig = mx_done[c]
            elif r == "ot":
                sig = oc_ready[c]
            else:
                sig = (p_ready if was[1] == XA else st_biased)[c]
            wait(eng, sig, was, it, same)

        def bank(step):
            r = RING_OF[step]
            return PS[r][:, RINGS[r].index(step) % NBANK[r], :]

        def passes(eng, body):
            body(-1, "A")
            body(0, "AB")
            with eng.Fori(1, NB - 1) as it:
                body(it, "ABT")
            body(NB - 1, "BT")
            body(NB, "T")

        def steps(phase):
            return [s for s in ORDER if CHAIN[s] in phase]

        def settle(eng):
            eng.sem_inc(settled[eng], 1)

        def col(name, c):
            return col_sb[:, COL[name] + c:COL[name] + c + 1]

        REL = [ENC, SA, CA]
        prw = PR[:].rearrange("p s n -> p (s n)")
        rel_sb = prw[0:H, 0:3 * 512].rearrange("h (r d e) -> h r d e", r=3, d=2)
        stage = [KM["B"][:].rearrange("p c v n -> p (c v n)"), prw[:, 4 * 512:8 * 512]]
        line = [b[0:H].rearrange("h c n -> h (c n)")[:, 0:LINE] for b in (XN["A"], XN["B"], OC["A"], OC["B"], XT, YT)]
        tables = []
        for a in REL:
            w = LK if a == ENC else LQ
            tables += [(tk[a], w, 0), (tq[a], w, P if a == ENC else 0)]
        flip = Y[:, 0, 0:P]
        N_ZEROED = 11
        HB = 8

        def block_heads(w):
            return 4 if w == LK else 2

        N_FLIP = sum(H // block_heads(w) for _, w, _ in tables)

        def bv_cols(a, c):
            return XT[:].rearrange("p c n -> p (c n)")[:, P * c:P * (c + 1)] if a % 2 == 0 else (
                YT[:].rearrange("p c n -> p (c n)")[:, P * c:P * (c + 1)])

        @block.sync
        def _(sp):
            for r in range(3):
                sp.dma_start(rel_sb[:, r, 0, :], rel_up[r]).then_inc(toep, 16)
                sp.dma_start(rel_sb[:, r, 1, :], rel_down[r]).then_inc(toep, 16)
            sp.wait_ge(built, 6)
            for i in range(6):
                sp.dma_start(lines[i], line[i]).then_inc(lines_out, 16)
            sp.wait_ge(lines_out, 96)
            n_load, turned = 0, []
            for j, (tab, w, off) in enumerate(tables):
                for h0 in range(0, H, HB):
                    if n_load >= 2:
                        sp.wait_ge(flip_out, turned[n_load - 2])
                    sp.dma_start(stage[n_load % 2][:, 0:HB * w].rearrange("p (h w) -> p h w", h=HB),
                                 bass.AP(lines.tensor, j * H * LINE + h0 * LINE + off,
                                         [[1, P], [LINE, HB], [1, w]])).then_inc(staged[n_load % 2], 16)
                    turned.append((turned[-1] if turned else 0) + HB // block_heads(w))
                    n_load += 1
            credit(sp, "sync")

            def body(it, phase):
                if "A" in phase:
                    wait(sp, full["A"], ("mem",), it, False)
                    settle(sp)
                    nb = it + 1
                    sp.dma_start(C[0:LK, :, :], ctxt[bass.ds(nb, 1)].rearrange("b k d -> k b d")).then_inc(c_loaded["sem"], 16)
                    wait(sp, xn_ready["A"], ("L0", TQ - 1), it, False)
                    settle(sp)
                    sp.dma_start(X[:], x[bass.ds(nb, 1)].rearrange("b (t p) d -> p (b t) d", p=P)).then_inc(x_loaded["sem"], 16)
                if "T" in phase:
                    nb = it - 1
                    wait(sp, dve_done["T"], ("f2", "B", TQ - 1), it)
                    settle(sp)
                    sp.dma_start(out[bass.ds(nb, 1)].rearrange("b (t p) d -> p (b t) d", p=P), Y[:]).then_inc(stored["sem"], 16)

            passes(sp, body)
            wait(sp, stored, "stored", NB)

        @block.tensor
        def _(pe):
            mm, tr = nc.tensor.matmul, nc.tensor.transpose
            pe.wait_ge(ident_made, 4)
            pe.wait_ge(head_mask_made, 2)
            pe.wait_ge(zeroed, N_ZEROED)
            pe.wait_ge(flip_made, 2)
            n_block = n_load = 0
            for tab, w, _ in tables:
                nh = block_heads(w)
                for h0 in range(0, H, HB):
                    pe.wait_ge(staged[n_load % 2], 16 * (n_load // 2 + 1))
                    for q in range(HB // nh):
                        n_block += 1
                        if n_block > 2:
                            pe.wait_ge(flip_out, n_block - 2)
                        mm(PS["gp"][:, n_block % 2, 0:nh * w], flip,
                           stage[n_load % 2][:, nh * w * q:nh * w * (q + 1)], start=True, stop=True).then_inc(flip_full, 1)
                    n_load += 1
            pe.wait_ge(flip_out, N_FLIP)
            pe.wait_ge(w_loaded, 80)
            for a in range(4):
                pe.wait_ge(bv_spread, a + 1)
                if a >= 2:
                    pe.wait_ge(bo_added, a - 1)
                for c in range(KC):
                    i = mm(PS["gp"][:, a % 2, 0:D], bv_cols(a, c), w_sb[:, 4 * a + 3, c, :], start=c == 0, stop=c == KC - 1)
                i.then_inc(bo_full, 1)
            pe.wait_ge(bo_added, 4)
            credit(pe, "tensor")

            def transposes(b_, src, nt, n_tiles):
                for c in range(KC):
                    for t in range(n_tiles):
                        at = nt * (n_tiles * c + t)
                        i = tr(b_[:, at:at + nt], src[0:nt, t, P * c:P * (c + 1)], ident[0:nt, 0:nt])
                return i

            def project(b_, w, src, n):
                for c in range(KC):
                    for k in range(KC):
                        i = mm(b_[:, n * c:n * (c + 1)], w[:, k, P * c:P * (c + 1)], src[:, k, 0:n],
                               start=k == 0, stop=k == KC - 1)
                return i

            def project_tokens(b_, w, src, nt, n_tiles, n_k=KC):
                for t in range(n_tiles):
                    for k in range(n_k):
                        i = mm(b_[0:nt, D * t:D * (t + 1)], src[:, k, nt * t:nt * (t + 1)], w[:, k, :],
                               start=k == 0, stop=k == n_k - 1)
                return i

            def body(it, phase):
                for s in steps(phase):
                    kind, ch = s[0], CHAIN[s]
                    if s not in RING_OF:
                        continue
                    a = s[1] if len(s) > 1 else None
                    b_ = bank(s)
                    if kind in ("q", "k", "v", "mt", "o", "mx", "st", "pv", "tq", "tc"):
                        nt = LK if a == ENC else P
                        nk = key_tile(a)
                        src_q = {ENC: ET, XA: XT, SA: YT, CA: YT}[a]
                        src_k = {ENC: ET, XA: CT, SA: YT, CA: MEMT}[a]
                    if kind == "ct":
                        wait(pe, c_loaded, "c_loaded", it)
                    elif kind == "xt":
                        wait(pe, x_loaded, "x_loaded", it)
                    elif kind == "et":
                        wait(pe, xn_ready["A"], ("E1" if a == ENC else "E2", 0), it)
                    elif kind == "yt":
                        wait(pe, xn_ready[ch], ({SA: "D1", CA: "D2", "ff": "D3"}[a], TQ - 1), it)
                    elif kind == "mem":
                        wait(pe, dve_done["A"], ("f2", "A", 0), it)
                    elif kind == "q":
                        wait(pe, act_done[ch], {ENC: ("et", ENC), XA: ("xt",), SA: ("yt", SA), CA: ("yt", CA)}[a], it)
                    elif kind == "k":
                        if a == CA:
                            wait(pe, act_done["A"], ("mem",), it, False)
                        else:
                            wait(pe, act_done[ch], {ENC: ("et", ENC), XA: ("ct",), SA: ("yt", SA)}[a], it)
                    elif kind == "mx" and s[2] == 0:
                        wait(pe, qr_ready[ch], ("q", a), it)
                        wait(pe, kr_ready[ch], (("k", a), KC - 1), it)
                    elif kind == "mt":
                        wait(pe, mx_done[ch], ("mx", a, len(max_tiles(a)) - 1), it)
                    elif kind == "st" and s[2] == 0:
                        wait(pe, act_done[ch], ("mt", a), it)
                    elif kind == "pv":
                        wait(pe, p_ready[ch], ("st", a, len(units(a)) * (s[2] + 1) // 4 - 1), it)
                        if s[2] == 0:
                            wait(pe, act_done[ch], ("v", a), it)
                    elif kind == "tq" and s[2] == 0:
                        wait(pe, oc_ready[ch], ("pv", a, 3), it)
                    elif kind == "tc":
                        wait(pe, dve_done[ch], ("tq", a, query_tiles(a) - 1), it)
                    elif kind == "o":
                        wait(pe, act_done[ch], ("tc", a), it)
                    elif kind == "f1" and s[2] == 0:
                        if ch == "A":
                            wait(pe, act_done["A"], ("et", "ff"), it)
                        else:
                            wait(pe, act_done["B"], ("yt", "ff"), it, False)
                    elif kind == "f2" and s[2] == 0:
                        wait(pe, act_done[ch], ("f1", a, 1 if ch == "A" else 3), it)
                    wait_place(pe, s, it, phase)
                    if kind == "ct" or kind == "mem":
                        i = transposes(b_, C, LK, 1)
                    elif kind == "xt":
                        i = transposes(b_, X, P, TQ)
                    elif kind == "et":
                        i = transposes(b_, XE, LK, 1)
                    elif kind == "yt":
                        i = transposes(b_, XN["B"], P, TQ)
                    elif kind == "q":
                        i = project(b_, w_sb[:, 4 * a], src_q, queries(a))
                    elif kind == "k":
                        i = project(b_, w_sb[:, 4 * a + 1], src_k, keys(a))
                    elif kind == "v":
                        i = project_tokens(b_, w_sb[:, 4 * a + 2], src_k, nk, keys(a) // nk)
                    elif kind == "mx":
                        t, g, v, nh, n_keys = max_tiles(a)[s[2]]
                        c, r = divmod(g, 2)
                        o = b_[0:nt, 0:nh * n_keys].rearrange("p (h k) -> p h k", h=nh)
                        if a != XA:
                            h0, j0 = 4 * g + v, 0 if a == ENC else P - P * t
                            mm(o, identb[0:nt, 0:nt], tq[a][0:nt, h0:h0 + nh, j0:j0 + n_keys], start=True, stop=False)
                        i = mm(o, QR[ch][:, c, r, P * t:P * t + nt], KR[ch][:, c, v:v + nh, 0:n_keys],
                               start=a == XA, stop=True)
                    elif kind == "mt":
                        for t in range(query_tiles(a)):
                            i = tr(b_[0:MR, P * t:P * t + nt], NM[ch][0:nt, t, :], ident[0:nt, 0:nt])
                    elif kind == "st":
                        g, v0, nh, kt, q0, nq = units(a)[s[2]]
                        c, r = divmod(g, 2)
                        for j in range(nh):
                            at = 64 * r + 4 * c + v0 + j
                            mm(b_[0:nk, nq * j:nq * (j + 1)], identb[:, at:at + 1].broadcast_to([P, nk]),
                               MT[ch][:, q0:q0 + nq], start=j == 0, stop=False)
                        for j in range(nh):
                            i = mm(b_[0:nk, nq * j:nq * (j + 1)], KM[ch][:, c, v0 + j, P * kt:P * kt + nk],
                                   QT[ch][:, c, r, q0:q0 + nq], start=False, stop=j == nh - 1)
                    elif kind == "pv":
                        us = [(u, x) for u, x in enumerate(units(a)) if x[0] == s[2]]
                        for kt in range(keys(a) // nk):
                            for v in range(4):
                                u, (_, v0, nh, _, q0, nq) = next(
                                    (u, x) for u, x in us if x[3] == kt and x[1] <= v < x[1] + x[2])
                                i = mm(b_[32 * v:32 * v + HD + 1, q0:q0 + nq], V[ch][0:nk, kt, 4 * s[2] + v, :],
                                       PR[0:nk, unit_slot(a, u), nq * (v - v0):nq * (v - v0 + 1)],
                                       start=kt == 0, stop=kt == keys(a) // nk - 1, tile_position=(0, 32 * v))
                    elif kind == "tq":
                        for g in range(4):
                            i = tr(b_[0:nt, P * g:P * (g + 1)], OC[ch][:, g, P * s[2]:P * s[2] + nt], ident[:])
                    elif kind == "tc":
                        i = transposes(b_, CN[ch], nt, query_tiles(a))
                    elif kind == "o":
                        i = project_tokens(b_, w_sb[:, 4 * a + 3], src_q, nt, query_tiles(a))
                    elif kind == "f1":
                        e, n = (0, LK) if ch == "A" else (1, LQ)
                        per = FC // 2 if ch == "A" else FC // 4
                        src = ET if ch == "A" else YT
                        for m in range(per):
                            for k in range(KC):
                                at = P * (per * s[2] + m)
                                i = mm(b_[:, n * m:n * (m + 1)], ff1_sb[:, e, k, at:at + P], src[:, k, :],
                                       start=k == 0, stop=k == KC - 1)
                    elif kind == "f2":
                        e, nt = (0, LK) if ch == "A" else (1, P)
                        i = project_tokens(b_, ff2_sb[:, e], HID[s[1]][:, :, nt * s[2]:nt * (s[2] + 1)], nt, 1, FC)
                    i.then_inc(full[ch]["sem"], 1)

            passes(pe, body)

        @block.scalar
        def _(act):
            copy = nc.scalar.copy
            act.dma_start(w_sb[:].rearrange("p m c n -> p m (c n)"), wm).then_inc(w_loaded, 16)
            act.dma_start(ff1_sb[:].rearrange("p m c n -> p m (c n)"), wff1).then_inc(w_loaded, 16)
            act.dma_start(ff2_sb[:].rearrange("p m c n -> p m (c n)"), wff2).then_inc(w_loaded, 16)
            act.dma_start(col_sb[:], cols).then_inc(w_loaded, 16)
            act.dma_start(row_sb[:].rearrange("p r d -> p (r d)"),
                          bass.AP(rows.tensor, 0, [[0, P], [1, len(ROWS) * D]])).then_inc(w_loaded, 16)
            n_block = 0
            for tab, w, _ in tables:
                nh = block_heads(w)
                for q in range(H // nh):
                    n_block += 1
                    act.wait_ge(flip_full, n_block)
                    copy(tab[:, nh * q:nh * (q + 1), :],
                         PS["gp"][:, n_block % 2, 0:nh * w].rearrange("p (h w) -> p h w", h=nh)).then_inc(flip_out, 1)
            act.wait_ge(w_loaded, 80)
            credit(act, "scalar")

            def affine_features(b_, dst, scale, bias):
                n = dst.shape[2]
                for c in range(KC):
                    i = nc.scalar.activation(dst[:, c, :], b_[:, n * c:n * (c + 1)], ACT.Identity, bias=col(bias, c),
                                             scale=col(scale, c))
                return i

            def body(it, phase):
                for s in steps(phase):
                    kind, ch = s[0], CHAIN[s]
                    a = s[1] if len(s) > 1 else None
                    if kind == "st":
                        g, v0, nh, kt, q0, nq = units(a)[s[2]]
                        dst = PR[0:key_tile(a), unit_slot(a, s[2]), 0:nh * nq]
                        src = dst
                        if a == XA:
                            wait(act, full[ch], s, it)
                            src = bank(s)[0:LK, 0:nh * nq]
                        else:
                            wait(act, st_biased[ch], s, it)
                        nc.scalar.activation(dst, src, ACT.Exp).then_inc(p_ready[ch]["sem"], 1)
                        continue
                    if kind == "pv":
                        wait(act, full[ch], s, it)
                        nq = queries(a)
                        copy(OC[ch][:, s[2], 0:nq], bank(s)[:, 0:nq]).then_inc(oc_ready[ch]["sem"], 1)
                        continue
                    if GENERAL.get(kind) != "act" and kind != "k":
                        continue
                    if kind == "k":
                        w = keys(a)
                        for c in range(KC):
                            wait(act, km_ready[ch], (s, c), it)
                            copy(KR[ch][:, c, :, 0:w], KM[ch][:, c, :, 0:w]).then_inc(kr_ready[ch]["sem"], 1)
                        continue
                    b_ = bank(s)
                    wait(act, full[ch], s, it)
                    if kind in ("ct", "xt", "mem", "tc"):
                        dst = {"ct": CT, "xt": XT, "mem": MEMT}.get(kind) or (ET if a == ENC else XT if a == XA else YT)
                        n = dst.shape[2]
                        if kind == "mem":
                            wait(act, full["B"], ("v", CA), it)
                        i = copy(dst[:].rearrange("p c n -> p (c n)"), b_[:, 0:KC * n])
                    elif kind == "et":
                        n = "1" if a == ENC else "2"
                        i = affine_features(b_, ET[:], f"enc_n{n}_s", f"enc_n{n}_b")
                    elif kind == "yt":
                        n = {SA: "1", CA: "2", "ff": "3"}[a]
                        i = affine_features(b_, YT[:], f"dec_n{n}_s", f"dec_n{n}_b")
                    elif kind == "q":
                        w = queries(a)
                        for c in range(KC):
                            for r in range(2):
                                half = slice(64 * r, 64 * r + 64)
                                i = nc.scalar.activation(QT[ch][half, c, r, 0:w], b_[half, w * c:w * (c + 1)], ACT.Identity,
                                                         bias=col(PRE[a] + "_bq", c)[half], scale=1.0)
                    elif kind == "v":
                        nk = key_tile(a)
                        n = keys(a) // nk
                        i = copy(V[ch][0:nk, 0:n, :, 0:HD], b_[0:nk, 0:D * n].rearrange("p (t h d) -> p t h d", t=n, h=H))
                    elif kind == "mt":
                        nq = queries(a)
                        i = copy(MT[ch][0:MR, 0:nq], b_[0:MR, 0:nq])
                    elif kind == "f1":
                        n, per = (LK, FC // 2) if ch == "A" else (LQ, FC // 4)
                        for m in range(per):
                            mi = per * s[2] + m
                            i = nc.scalar.activation(HID[s[1]][:, mi, :], b_[:, n * m:n * (m + 1)], ACT.Relu,
                                                     bias=col("enc_ff1" if ch == "A" else "dec_ff1", mi), scale=1.0)
                    i.then_inc(act_done[ch]["sem"], 1)

            passes(act, body)

        @block.vector
        def _(dve):
            tt, ts, cp = nc.vector.tensor_tensor, nc.vector.tensor_scalar, nc.vector.tensor_copy
            for c in "AB":
                nc.vector.memset(NM[c][:], 0.0).then_inc(zeroed, 1)
                nc.vector.memset(V[c][:], 1.0).then_inc(zeroed, 1)
                nc.vector.memset(MT[c][:], 0.0).then_inc(zeroed, 1)
                nc.vector.memset(QT[c][:], 0.0).then_inc(zeroed, 1)
                nc.vector.memset(QR[c][:], 0.0).then_inc(zeroed, 1)
            nc.vector.memset(PS["ot"][:], 0.0).then_inc(zeroed, 1)
            dve.wait_ge(toep, 96)
            for r in range(3):
                up, down = rel_sb[:, r, 0, :], rel_sb[:, r, 1, :]
                lk_, lq_ = line[2 * r], line[2 * r + 1]
                far = up[:, P - 1:P]
                if REL[r] == SA:
                    cp(lk_[:, P - 1:P], down[:, P - 1:P])
                    nc.vector.memset(lk_[:, 0:P - 1], MASKED)
                else:
                    cp(lk_[:, 0:P], down[:, 0:P])
                cp(lk_[:, P:2 * P - 1], up[:, 1:P])
                cp(lk_[:, 2 * P - 1:LINE], far.broadcast_to([H, LINE - 2 * P + 1])).then_inc(built, 1)
                cp(lq_[:, 0:P], far.broadcast_to([H, P]))
                cp(lq_[:, P:2 * P - 1], down[:, P:2 * P - 1])
                if REL[r] == SA:
                    nc.vector.memset(lq_[:, 2 * P:LINE], MASKED)
                    cp(lq_[:, 2 * P - 1:2 * P], up[:, P:P + 1]).then_inc(built, 1)
                else:
                    nc.vector.memset(lq_[:, LINE - 1:LINE], 0.0)
                    cp(lq_[:, 2 * P - 1:LINE - 1], up[:, P:2 * P]).then_inc(built, 1)
            dve.wait_ge(ident_made, 3)
            cp(identb[:], ident[:]).then_inc(ident_made, 1)
            dve.wait_ge(ident_made, 4)
            nc.vector.tensor_reduce(head_mask[:], ident[:].rearrange("p (r v d) -> p v r d", r=2, v=4), AX.XY,
                                    ALU.add).then_inc(head_mask_made, 1)
            dve.wait_ge(head_mask_made, 1)
            ts(head_mask[:], head_mask[:], SCALE, None, ALU.mult).then_inc(head_mask_made, 1)
            dve.wait_ge(head_mask_made, 2)
            dve.wait_ge(w_loaded, 80)
            dve.wait_ge(flip_out, N_FLIP)
            for a in range(4):
                if a >= 2:
                    dve.wait_ge(bo_full, a - 1)
                for c in range(KC):
                    i = cp(bv_cols(a, c), col(PRE[a] + "_bv", c).broadcast_to([P, P]))
                i.then_inc(bv_spread, 1)
            for a in range(4):
                dve.wait_ge(bo_full, a + 1)
                bo = row_sb[:, ROW[PRE[a] + "_bo"], :]
                tt(bo, PS["gp"][:, a % 2, 0:D], bo, ALU.add).then_inc(bo_added, 1)
            dve.wait_ge(zeroed, N_ZEROED)
            credit(dve, "vector")

            def buffers(l):
                return {"E": (C, XE, LK), "L": (X, XN["A"], P), "D": (XN["A"] if l == "D1" else Y, XN["B"], P)}[l[0]]

            def moments(l, ch, it):
                src, _, np_ = buffers(l)
                source = {"E1": (c_loaded, "c_loaded"), "E2": (dve_done["A"], ("o", ENC)), "L0": (dve_done["A"], ("o", XA)),
                          "D1": (affine, "beta"), "D2": (dve_done["B"], ("o", SA)), "D3": (dve_done["B"], ("o", CA))}[l]
                wait(dve, *source, it, l != "D1")
                for t in range(ln_tiles[l]):
                    nc.vector.bn_stats(st6[ch][0:np_, t, :], src[0:np_, t, :]).then_inc(stats[ch]["sem"], 1)
                wait(dve, stats[ch], (l, ln_tiles[l] - 1), it)
                settle(dve)
                for t in range(ln_tiles[l]):
                    nc.vector.bn_aggr(mv[ch][0:np_, t, :], st6[ch][0:np_, t, :]).then_inc(aggr[ch]["sem"], 1)

            def normalise(l, ch, it):
                src, dst, np_ = buffers(l)
                if l == "D1":
                    wait(dve, full["B"], ("yt", "ff"), it, False)
                wait(dve, rstd_ready[ch], l, it)
                for t in range(ln_tiles[l]):
                    ts(dst[0:np_, t, :], src[0:np_, t, :], mv[ch][0:np_, t, 0:1], rstd[ch][0:np_, t:t + 1],
                       ALU.subtract, ALU.mult).then_inc(xn_ready[ch]["sem"], 1)

            def body(it, phase):
                for s in steps(phase):
                    kind, ch = s[0], CHAIN[s]
                    a = s[1] if len(s) > 1 else None
                    if kind == "affine":
                        gam = row_sb[:, ROW["gamma"]:ROW["gamma"] + 1, :].broadcast_to([P, TQ, D])
                        bet = row_sb[:, ROW["beta"]:ROW["beta"] + 1, :].broadcast_to([P, TQ, D])
                        wait(dve, xn_ready["A"], ("L0", TQ - 1), it)
                        tt(XN["A"][:], XN["A"][:], gam, ALU.mult).then_inc(affine["sem"], 1)
                        wait(dve, affine, "gamma", it)
                        tt(XN["A"][:], XN["A"][:], bet, ALU.add).then_inc(affine["sem"], 1)
                    elif kind == "ln":
                        moments(a, ch, it)
                    elif kind == "nx":
                        normalise(a, ch, it)
                    elif kind == "mx":
                        t, g, v, nh, n_keys = max_tiles(a)[s[2]]
                        c, r = divmod(g, 2)
                        nt, at = LK if a == ENC else P, 64 * r + 4 * c + v
                        wait(dve, full[ch], s, it)
                        nc.vector.tensor_reduce(NM[ch][0:nt, t, at:at + nh],
                                                bank(s)[0:nt, 0:nh * n_keys].rearrange("p (h k) -> p h k", h=nh),
                                                AX.X, ALU.max, negate=True).then_inc(mx_done[ch]["sem"], 1)
                    elif kind == "st" and a != XA:
                        g, v0, nh, kt, q0, nq = units(a)[s[2]]
                        nk, h0 = key_tile(a), 4 * g + v0
                        wait(dve, full[ch], s, it)
                        tt(PR[0:nk, unit_slot(a, s[2]), 0:nh * nq].rearrange("p (h q) -> p h q", h=nh),
                           bank(s)[0:nk, 0:nh * nq].rearrange("p (h q) -> p h q", h=nh),
                           tk[a][0:nk, h0:h0 + nh, 0:nq], ALU.add).then_inc(st_biased[ch]["sem"], 1)
                    elif kind == "q":
                        w = queries(a)
                        wait(dve, act_done[ch], s, it)
                        cp(QR[ch][:, :, :, 0:w], QT[ch][:, :, :, 0:w]).then_inc(qr_ready[ch]["sem"], 1)
                    elif GENERAL.get(kind, "act") != "act":
                        b_ = bank(s)
                        wait(dve, full[ch], s, it)
                        if kind == "k":
                            w = keys(a)
                            for c in range(KC):
                                for v in range(4):
                                    i = ts(KM[ch][:, c, v, 0:w], b_[:, w * c:w * (c + 1)], col(PRE[a] + "_bk", c),
                                           head_mask[:, v:v + 1], ALU.add, ALU.mult)
                                i.then_inc(km_ready[ch]["sem"], 1)
                            continue
                        elif kind == "tq":
                            nt = LK if a == ENC else P
                            tqs = of(ch, ["tq"])
                            n = tqs.index(s)
                            rd = rden[ch][0:nt, n % 2, :].rearrange("p (h o) -> p h o", o=1)
                            o = b_[0:nt, :].rearrange("p (h d) -> p h d", d=32)
                            if n >= 2:
                                wait(dve, dve_done[ch], tqs[n - 2], it)
                            else:
                                prev = [x for i_, x in enumerate(tqs) if i_ % 2 == n % 2][-1]
                                wait(dve, dve_done[ch], prev, it, False)
                            if ch == "A" and n == 0:
                                wait(dve, pre_added["B"], "sa_bo", it)
                            nc.vector.reciprocal(rd, o[:, :, HD:HD + 1]).then_inc(den_ready[ch]["sem"], 1)
                            wait(dve, den_ready[ch], s, it)
                            i = tt(CN[ch][0:nt, s[2], :].rearrange("p (h d) -> p h d", h=H), o[:, :, 0:HD],
                                   rd.broadcast_to([nt, H, HD]), ALU.mult)
                        elif kind in ("o", "f2"):
                            name = PRE[a] + "_bo" if kind == "o" else ("enc_ff2" if ch == "A" else "dec_ff2")
                            wait(dve, pre_added["A" if ch == "A" else "B"], name, it, ch != "T")
                            dst = C[0:LK, :, :] if a in (ENC, "A") else X[:] if a == XA else Y[:]
                            if s[0:2] == ("f2", "B"):
                                dst = Y[:, s[2]:s[2] + 1, :]
                            np_, n_t, _ = dst.shape
                            i = tt(dst, b_[0:np_, 0:n_t * D].rearrange("p (t d) -> p t d", t=n_t), dst, ALU.add)
                        i.then_inc(dve_done[ch]["sem"], 1)

            passes(dve, body)

        @block.gpsimd
        def _(pool):
            nc.gpsimd.memset(ident[:], 0.0).then_inc(ident_made, 1)
            pool.wait_ge(ident_made, 1)
            nc.gpsimd.affine_select(out=ident[:], in_=ident[:], compare_op=ALU.not_equal, fill=1.0, base=0,
                                    pattern=[[-1, P]], channel_multiplier=1).then_inc(ident_made, 1)
            nc.gpsimd.memset(exponent[:], -0.5).then_inc(ident_made, 1)
            nc.gpsimd.memset(flip, 0.0).then_inc(flip_made, 1)
            pool.wait_ge(flip_made, 1)
            nc.gpsimd.affine_select(out=flip, in_=flip, compare_op=ALU.not_equal, fill=1.0, base=1 - P,
                                    pattern=[[1, P]], channel_multiplier=1).then_inc(flip_made, 1)
            pool.wait_ge(ident_made, 3)
            pool.wait_ge(w_loaded, 80)
            credit(pool, "gpsimd")

            def inverse_deviation(l, ch, it):
                n_t, np_ = ln_tiles[l], LK if l[0] == "E" else P
                eps = EPS_L0 if l == "L0" else EPS_L1
                wait(pool, aggr[ch], (l, n_t - 1), it)
                settle(pool)
                nc.gpsimd.tensor_scalar(ve[ch][0:np_, 0:n_t], mv[ch][0:np_, 0:n_t, 1], eps, 1.0, ALU.add,
                                        ALU.mult).then_inc(eps_added[ch]["sem"], 1)
                wait(pool, eps_added[ch], l, it)
                nc.gpsimd.tensor_tensor(rstd[ch][0:np_, 0:n_t], ve[ch][0:np_, 0:n_t], exponent[0:np_, 0:n_t],
                                        ALU.pow).then_inc(rstd_ready[ch]["sem"], 1)

            def add_row(name, dst, ch, src=None):
                np_, n_t, _ = dst.shape
                r = row_sb[0:np_, ROW[name]:ROW[name] + 1, :].broadcast_to([np_, n_t, D])
                nc.gpsimd.tensor_tensor(dst, dst if src is None else src, r, ALU.add).then_inc(pre_added[ch]["sem"], 1)

            def body(it, phase):
                for s in steps(phase):
                    kind, ch = s[0], CHAIN[s]
                    a = s[1] if len(s) > 1 else None
                    if kind == "ln":
                        inverse_deviation(a, ch, it)
                    elif kind == "q":
                        if a == ENC:
                            wait(pool, full["A"], ("ct",), it)
                            wait(pool, xn_ready["A"], ("E1", 0), it)
                            add_row("enc_bo", C[0:LK, :, :], ch)
                        elif a == XA:
                            wait(pool, xn_ready["A"], ("E2", 0), it)
                            add_row("enc_ff2", C[0:LK, :, :], ch)
                            wait(pool, full["A"], ("xt",), it)
                            add_row("xa_bo", X[:], ch)
                        elif a == SA:
                            wait(pool, affine, "beta", it, False)
                            wait(pool, stored, "stored", it)
                            add_row("sa_bo", Y[:], ch, XN["A"][:])
                        else:
                            wait(pool, xn_ready["B"], ("D2", TQ - 1), it)
                            add_row("ca_bo", Y[:], ch)
                    elif s == ("yt", "ff"):
                        wait(pool, xn_ready["B"], ("D3", TQ - 1), it)
                        add_row("dec_ff2", Y[:], ch)

            passes(pool, body)


def kernel(**inputs):
    import numpy as _np
    import concourse.bacc as _bacc
    from concourse import mybir as _mybir
    from concourse.bass_utils import run_bass_kernel_spmd as _run

    i = {k: _np.asarray(v) for k, v in inputs.items()}
    l0 = lambda k: i["L0_xattn_" + k]
    l1 = lambda k: i["L1_xattn_" + k]
    in_w = [l1("enc_in_w"), None, l1("dec_sa_in_w"), l1("dec_ca_in_w")]
    out_w = [l1("enc_out_w"), None, l1("dec_sa_out_w"), l1("dec_ca_out_w")]
    in_b = [l1("enc_in_b"), _np.concatenate([l0("bq"), l0("bk"), l0("bv")]), l1("dec_sa_in_b"), l1("dec_ca_in_b")]
    out_b = [l1("enc_out_b"), l0("bo"), l1("dec_sa_out_b"), l1("dec_ca_out_b")]
    mats = []
    for a in range(4):
        if in_w[a] is None:
            mats += [l0("Wq"), l0("Wk"), l0("Wv"), l0("Wo")]
        else:
            mats += [in_w[a][D * j:D * (j + 1)].T for j in range(3)] + [out_w[a].T]

    def chunks(m):
        return m.reshape(-1, P, m.shape[1]).transpose(1, 0, 2).reshape(P, -1)

    wm = _np.stack([chunks(m) for m in mats], 1)
    wff1 = _np.stack([chunks(l1("enc_ff1_w").T), chunks(l1("dec_ff1_w").T)], 1)
    wff2 = _np.stack([chunks(l1("enc_ff2_w").T), chunks(l1("dec_ff2_w").T)], 1)
    vecs = {}
    for a, p in enumerate(PRE):
        vecs[p + "_bq"], vecs[p + "_bk"], vecs[p + "_bv"] = (in_b[a][D * j:D * (j + 1)] for j in range(3))
        vecs[p + "_bo"] = out_b[a]
    for k in ("enc_n1", "enc_n2", "dec_n1", "dec_n2", "dec_n3"):
        vecs[k + "_s"], vecs[k + "_b"] = l1(k + "_s"), l1(k + "_b")
    vecs["gamma"], vecs["beta"] = l0("ln_gamma"), l0("ln_beta")
    vecs["enc_ff2"], vecs["dec_ff2"] = l1("enc_ff2_b"), l1("dec_ff2_b")
    cols = _np.concatenate([vecs[k].reshape(-1, P).T for k in COLS]
                           + [l1("enc_ff1_b").reshape(-1, P).T, l1("dec_ff1_b").reshape(-1, P).T], 1)
    rows = _np.stack([vecs[k] for k in ROWS])
    rels = [l1("enc_rel"), l1("dec_rel_self"), l1("dec_rel_cross")]
    arrays = {"x": i["x"], "ctxt": i["ctx_1024"], "wm": wm, "wff1": wff1, "wff2": wff2, "cols": cols, "rows": rows,
              "rel_up": _np.stack([r.T for r in rels]), "rel_down": _np.stack([r[::-1].T for r in rels])}
    nc = _bacc.Bacc("TRN2", target_bir_lowering=False, num_devices=1)
    feed, args = {}, []
    for name, a in arrays.items():
        a = _np.ascontiguousarray(a)
        feed[f"in_{name}"] = a
        args.append(nc.dram_tensor(f"in_{name}", a.shape, _mybir.dt.from_np(a.dtype), kind="ExternalInput").ap())
    args.append(nc.dram_tensor("out_0", (NB, LQ, D), _mybir.dt.float32, kind="ExternalOutput").ap())
    build(nc, *args)
    r = _run(nc, [feed], core_ids=[0])
    return r.results[0]["out_0"]
```
